# Optimizing a Trainium2 kernel written in Bass

```python
import numpy as np
import jax
import jax.numpy as jnp

def _softmax(x, axis=-1):
    return jax.nn.softmax(x, axis=axis)

def _gelu(x):
    return jax.nn.gelu(x, approximate=True)

def _silu(x):
    return jax.nn.silu(x)

def _sigmoid(x):
    return jax.nn.sigmoid(x)

def _layernorm(x, axis=-1, eps=1e-05):
    m = jnp.mean(x, axis=axis, keepdims=True)
    v = jnp.var(x, axis=axis, keepdims=True)
    return (x - m) / jnp.sqrt(v + eps)

def _scatter_add(tgt, idx, src, axis=0):
    return tgt.at[idx].add(src)

def _segment_sum(src, seg, n):
    return jax.ops.segment_sum(src, seg, n)
kernel_name = 'mk_seq_postln_d1_jaxref_r4_bbb881'

def setup_inputs(seed: int=0):
    np.random.seed(seed)
    _w = jnp.asarray

    def _L0_attn_setup():
        import jax, jax.numpy as jnp
        import numpy as np
        D_MODEL, D_STATE, D_CONV, EXPAND = (256, 16, 4, 2)
        D_INNER = EXPAND * D_MODEL
        DT_RANK = D_INNER // 16
        BATCH, SEQ = (1, 512)

        def _causal_depthwise_conv(u, conv_w, conv_b):
            B, L, Di = u.shape
            K = conv_w.shape[1]
            up = jnp.pad(u, ((0, 0), (K - 1, 0), (0, 0)))
            y = jnp.zeros_like(u)
            for k in range(K):
                y = y + up[:, k:k + L, :] * conv_w[:, k]
            return y + conv_b

        def _selective_scan(u, dt, A, Bm, Cm, D_param):
            dA = jnp.exp(dt[..., None] * A)
            dBu = (dt * u)[..., None] * Bm[:, :, None, :]

            def step(h, inp):
                dA_t, dBu_t, C_t = inp
                h = dA_t * h + dBu_t
                y = jnp.einsum('bdn,bn->bd', h, C_t)
                return (h, y)
            h0 = jnp.zeros((u.shape[0], u.shape[2], A.shape[1]), u.dtype)
            _, ys = jax.lax.scan(step, h0, (jnp.moveaxis(dA, 1, 0), jnp.moveaxis(dBu, 1, 0), jnp.moveaxis(Cm, 1, 0)))
            y = jnp.moveaxis(ys, 0, 1)
            return y + u * D_param
        key = jax.random.key(seed)
        ks = jax.random.split(key, 8)
        s = lambda k, shape, sc: jax.random.normal(k, shape, jnp.float32) * sc
        x = s(ks[0], (BATCH, SEQ, D_MODEL), 1.0)
        W_in = s(ks[1], (D_MODEL, 2 * D_INNER), 0.02)
        conv_w = s(ks[2], (D_INNER, D_CONV), 0.1)
        conv_b = jnp.zeros((D_INNER,), jnp.float32)
        W_x = s(ks[3], (D_INNER, DT_RANK + 2 * D_STATE), 0.02)
        W_dt = s(ks[4], (DT_RANK, D_INNER), 0.02)
        b_dt = s(ks[5], (D_INNER,), 0.1)
        A_log = jnp.log(jnp.tile(jnp.arange(1, D_STATE + 1, dtype=jnp.float32)[None, :], (D_INNER, 1)))
        D_param = jnp.ones((D_INNER,), jnp.float32)
        W_out = s(ks[6], (D_INNER, D_MODEL), 0.02)
        return dict(x=x, W_in=W_in, conv_w=conv_w, conv_b=conv_b, W_x=W_x, W_dt=W_dt, b_dt=b_dt, A_log=A_log, D_param=D_param, W_out=W_out)
    _L0_attn_in = _L0_attn_setup()

    def _L0_ffn_setup():
        import jax, jax.numpy as jnp
        import numpy as np
        import math
        B, L, D = (4, 1024, 256)
        F = 1024
        E = 16
        CAP_FACTOR = 1.0
        EPS = 1e-05
        key = jax.random.key(seed)
        ks = jax.random.split(key, 8)
        std = 0.02
        return {'x': jax.random.normal(ks[0], (B, L, D), dtype=jnp.float32), 'norm_weight': jnp.ones((D,), dtype=jnp.float32), 'router_weight': jax.random.normal(ks[1], (E, D), dtype=jnp.float32) * std, 'router_bias': jnp.zeros((E,), dtype=jnp.float32), 'fc1_weight': jax.random.normal(ks[2], (E, F, D), dtype=jnp.float32) * std, 'fc1_bias': jnp.zeros((E, F), dtype=jnp.float32), 'fc2_weight': jax.random.normal(ks[3], (E, D, F), dtype=jnp.float32) * std, 'fc2_bias': jnp.zeros((E, D), dtype=jnp.float32)}
    _L0_ffn_in = _L0_ffn_setup()
    _d = {'L0_attn_x': _L0_attn_in['x'], 'L0_attn_W_in': _L0_attn_in['W_in'], 'L0_attn_conv_w': _L0_attn_in['conv_w'], 'L0_attn_conv_b': _L0_attn_in['conv_b'], 'L0_attn_W_x': _L0_attn_in['W_x'], 'L0_attn_W_dt': _L0_attn_in['W_dt'], 'L0_attn_b_dt': _L0_attn_in['b_dt'], 'L0_attn_A_log': _L0_attn_in['A_log'], 'L0_attn_D_param': _L0_attn_in['D_param'], 'L0_attn_W_out': _L0_attn_in['W_out'], 'L0_ffn_norm_weight': _L0_ffn_in['norm_weight'], 'L0_ffn_router_weight': _L0_ffn_in['router_weight'], 'L0_ffn_router_bias': _L0_ffn_in['router_bias'], 'L0_ffn_fc1_weight': _L0_ffn_in['fc1_weight'], 'L0_ffn_fc1_bias': _L0_ffn_in['fc1_bias'], 'L0_ffn_fc2_weight': _L0_ffn_in['fc2_weight'], 'L0_ffn_fc2_bias': _L0_ffn_in['fc2_bias']}
    _x0 = _d['L0_attn_x']
    _d['L0_attn_x'] = jax.random.normal(jax.random.fold_in(jax.random.key(seed), 1), (8, 2048, 256), dtype=_x0.dtype)
    del _x0
    return _d

def reference(L0_attn_x, L0_attn_W_in, L0_attn_conv_w, L0_attn_conv_b, L0_attn_W_x, L0_attn_W_dt, L0_attn_b_dt, L0_attn_A_log, L0_attn_D_param, L0_attn_W_out, L0_ffn_norm_weight, L0_ffn_router_weight, L0_ffn_router_bias, L0_ffn_fc1_weight, L0_ffn_fc1_bias, L0_ffn_fc2_weight, L0_ffn_fc2_bias):

    def _L0_attn_ref(x, W_in, conv_w, conv_b, W_x, W_dt, b_dt, A_log, D_param, W_out):
        import jax, jax.numpy as jnp
        import numpy as np
        D_MODEL, D_STATE, D_CONV, EXPAND = (256, 16, 4, 2)
        D_INNER = EXPAND * D_MODEL
        DT_RANK = D_INNER // 16
        BATCH, SEQ = (1, 512)

        def _causal_depthwise_conv(u, conv_w, conv_b):
            B, L, Di = u.shape
            K = conv_w.shape[1]
            up = jnp.pad(u, ((0, 0), (K - 1, 0), (0, 0)))
            y = jnp.zeros_like(u)
            for k in range(K):
                y = y + up[:, k:k + L, :] * conv_w[:, k]
            return y + conv_b

        def _selective_scan(u, dt, A, Bm, Cm, D_param):
            dA = jnp.exp(dt[..., None] * A)
            dBu = (dt * u)[..., None] * Bm[:, :, None, :]

            def step(h, inp):
                dA_t, dBu_t, C_t = inp
                h = dA_t * h + dBu_t
                y = jnp.einsum('bdn,bn->bd', h, C_t)
                return (h, y)
            h0 = jnp.zeros((u.shape[0], u.shape[2], A.shape[1]), u.dtype)
            _, ys = jax.lax.scan(step, h0, (jnp.moveaxis(dA, 1, 0), jnp.moveaxis(dBu, 1, 0), jnp.moveaxis(Cm, 1, 0)))
            y = jnp.moveaxis(ys, 0, 1)
            return y + u * D_param
        proj = x @ W_in
        u, z = jnp.split(proj, 2, axis=-1)
        uc = jax.nn.silu(_causal_depthwise_conv(u, conv_w, conv_b))
        xdbc = uc @ W_x
        dt_r, Bm, Cm = jnp.split(xdbc, [DT_RANK, DT_RANK + D_STATE], axis=-1)
        dt = jax.nn.softplus(dt_r @ W_dt + b_dt)
        A = -jnp.exp(A_log)
        y = _selective_scan(uc, dt, A, Bm, Cm, D_param)
        y = y * jax.nn.silu(z)
        return y @ W_out

    def _L0_ffn_ref(x, norm_weight, router_weight, router_bias, fc1_weight, fc1_bias, fc2_weight, fc2_bias):
        import jax, jax.numpy as jnp
        import numpy as np
        import math
        B, L, D = (4, 1024, 256)
        F = 1024
        E = 16
        CAP_FACTOR = 1.0
        EPS = 1e-05
        b, l, d = x.shape
        n_tokens = b * l
        n_experts = router_weight.shape[0]
        capacity = max(1, math.ceil(CAP_FACTOR * n_tokens / n_experts))
        top_k = min(capacity, n_tokens)
        xf = x.reshape(n_tokens, d)
        rms = jnp.sqrt(jnp.mean(xf * xf, axis=-1, keepdims=True) + EPS)
        xn = xf / rms * norm_weight
        logits = xn @ router_weight.T + router_bias
        probs = jax.nn.softmax(logits, axis=-1)
        _, idx = jax.lax.top_k(logits.T, top_k)
        xe = xn[idx]
        h = jnp.einsum('ecd,efd->ecf', xe, fc1_weight) + fc1_bias[:, None, :]
        h = jax.nn.gelu(h, approximate=False)
        y = jnp.einsum('ecf,edf->ecd', h, fc2_weight) + fc2_bias[:, None, :]
        gates = jnp.take_along_axis(probs.T, idx, axis=1)
        flat_idx = idx.reshape(-1)
        contrib = (y * gates[:, :, None]).reshape(-1, d)
        output = jnp.zeros((n_tokens, d), dtype=x.dtype).at[flat_idx].add(contrib)
        gate_sums = jnp.zeros((n_tokens, 1), dtype=x.dtype).at[flat_idx].add(gates.reshape(-1, 1))
        assigned = gate_sums > 0
        output = jnp.where(assigned, output / jnp.where(assigned, gate_sums, 1.0), output)
        return output.reshape(b, l, d)
    x = L0_attn_x
    x = _layernorm(x + _L0_attn_ref(x, L0_attn_W_in, L0_attn_conv_w, L0_attn_conv_b, L0_attn_W_x, L0_attn_W_dt, L0_attn_b_dt, L0_attn_A_log, L0_attn_D_param, L0_attn_W_out), axis=-1)
    x = _layernorm(x + _L0_ffn_ref(x, L0_ffn_norm_weight, L0_ffn_router_weight, L0_ffn_router_bias, L0_ffn_fc1_weight, L0_ffn_fc1_bias, L0_ffn_fc2_weight, L0_ffn_fc2_bias), axis=-1)
    return x

_drawn_inputs = setup_inputs


def setup_inputs(seed=0):
    import zlib

    import numpy as np

    out = dict(_drawn_inputs(seed))
    spreads = {'L0_attn_conv_b': (0.0, 0.773),
     'L0_attn_D_param': (1.0, 0.6),
     'L0_ffn_norm_weight': (1.0, 0.2),
     'L0_ffn_router_bias': (0.0, 2.0),
     'L0_ffn_fc1_bias': (0.0, 0.321),
     'L0_ffn_fc2_bias': (0.0, 0.1)}
    factors = {'L0_attn_W_in': 5.869,
     'L0_attn_conv_w': 7.785,
     'L0_attn_W_x': 8.0,
     'L0_attn_W_dt': 8.0,
     'L0_attn_b_dt': 8.0,
     'L0_attn_A_log': 8.0,
     'L0_attn_W_out': 5.565}
    for name, (base, spread) in spreads.items():
        noise = np.random.default_rng([zlib.crc32(name.encode()), seed]).standard_normal(out[name].shape)
        drawn = base * np.exp(spread * noise) if base else spread * noise
        out[name] = jnp.asarray(drawn.astype(out[name].dtype))
    for name, factor in factors.items():
        out[name] = (out[name] * factor).astype(out[name].dtype)
    return out
```

```python
from contextlib import ExitStack

import numpy as np

import concourse.bass as bass
from concourse import mybir

P = 128
CH = 512
Q = CH // P
EPS = 1e-5
F32, BF16, I32, U32 = mybir.dt.float32, mybir.dt.bfloat16, mybir.dt.int32, mybir.dt.uint32
ALU, ACT, AX = mybir.AluOpType, mybir.ActivationFunctionType, mybir.AxisListType
DP = 96


class Count:

    def __init__(self, reg, per, base):
        self.reg, self.per, self.base = reg, per, base

    def __mul__(self, k):
        return Count(self.reg, self.per * k, self.base * k)

    def __add__(self, k):
        return Count(self.reg, self.per, self.base + k)

    def value(self):
        return self.base if self.per == 0 else self.reg * self.per + self.base


def wait(eng, sem, count):
    if isinstance(count, int):
        count = Count(None, 0, count)
    assert count.per == 0 or count.base >= 1
    if count.per or count.base > 0:
        eng.wait_ge(sem, count.value())


def mamba_phase(nc, d):
    NCH = d["x"].shape[0] // CH - 1
    N = d["A_log"].shape[1]
    D = d["x"].shape[1]
    KD = D // P
    DI = d["W_out"].shape[0]
    M = DI // P
    R = d["W_dt"].shape[0]
    E = d["router_bias"].shape[0]
    TAPS = d["conv_w"].shape[1]
    assert M == 4 and KD == 2 and R == 32 and N == 16 and TAPS == 4 and E * Q <= P
    assert NCH % 2 == 0 and d["seq"] == 4 * CH

    with ExitStack() as ctx:
        def sb(name, shape, dt=F32):
            return ctx.enter_context(nc.sbuf_tensor("sb_" + name, shape, dt))

        def sem(name):
            return ctx.enter_context(nc.semaphore(name))

        w_in = sb("w_in", [P, KD, 2 * DI])
        w_x = sb("w_x", [P, M, DP + R])
        w_dt = sb("w_dt", [P, DI])
        w_out = sb("w_out", [P, M, D])
        w_r = sb("w_r", [P, KD, E])
        conv_w = sb("conv_w", [P, M, TAPS])
        conv_b = sb("conv_b", [P, M])
        b_dt = sb("b_dt", [P, M])
        a_neg = sb("a_neg", [P, M, N])
        d_par = sb("d_par", [P, M])
        d_diag = sb("d_diag", [P, M, P])
        ident = sb("ident", [P, P])
        pick = sb("pick", [DP, 2 * N, P], BF16)
        nw_row = sb("nw_row", [P, D])
        rb_row = sb("rb_row", [P, E])
        neg_half = sb("neg_half", [P, 2 * Q])
        zeros = sb("zeros", [P, D + 1])
        keep = sb("keep", [P, N * M], I32)
        xT = sb("xT", [P, KD, CH])
        u = sb("u", [P, M, CH + TAPS - 1])
        halo = sb("halo", [P, M, TAPS - 1])
        work = sb("work", [P, M, CH])
        uc = sb("uc", [P, M, CH])
        sz = sb("sz", [P, 2, M, CH])
        dt = sb("dt", [P, 2, M, CH])
        dtu = sb("dtu", [P, 2, M, CH])
        bc = sb("bc", [DP, 2, CH], BF16)
        bc_rest = sb("bc_rest", [DP, CH])
        bc_mid = sb("bc_mid", [DP, CH], BF16)
        dt_r = sb("dt_r", [P, CH])
        b_row = sb("b_row", [P, 2, CH])
        c_row = sb("c_row", [P, 4, CH])
        da = sb("da", [P, 2, M, CH])
        h = sb("h", [P, 4, M, CH])
        hc = sb("hc", [P, 2, M, CH])
        state = sb("state", [P, N, M])
        xk = sb("xk", [P, Q, D])
        x1 = sb("x1", [P, Q, D])
        row = sb("row", [P, Q, D + E])
        xnT = sb("xnT", [P, KD, CH])
        stats = sb("stats", [P, Q, 6])
        mv = sb("mv", [P, Q, 2])
        var_e = sb("var_e", [P, 2, Q])
        rvar = sb("rvar", [P, Q])
        rms = sb("rms", [P, Q])
        scales = sb("scales", [P, 2, Q])
        lg_wide = sb("lg_wide", [P, P])
        lg = lg_wide[:, 0:Q * E].rearrange("p (q e) -> p q e", q=Q)
        lg_max = sb("lg_max", [P, Q])
        lg_d = sb("lg_d", [P, Q, E])
        lg_e = sb("lg_e", [P, Q, E])
        lg_s = sb("lg_s", [P, Q])
        lg_r = sb("lg_r", [P, Q])
        lgT = sb("lgT", [Q * E, P])

        y_ps = ctx.enter_context(nc.psum_tensor("y_ps", [P, M, CH], F32))
        bc_ps = ctx.enter_context(nc.psum_tensor("bc_ps", [P, 2, CH], F32))
        f_ps = ctx.enter_context(nc.psum_tensor("f_ps", [P, 2, CH], F32))

        weights_in = sem("weights_in")
        set_up = sem("set_up")
        a_ready = sem("a_ready")
        xT_in, xk_in, stored, zeroed = sem("xT_in"), sem("xk_in"), sem("stored"), sem("zeroed")
        store_free = sem("store_free")
        u_made, u_copied, conv_ops, uc_made = sem("u_made"), sem("u_copied"), sem("conv_ops"), sem("uc_made")
        halo_put, halo_saved = sem("halo_put"), sem("halo_saved")
        z_made, z_done = sem("z_made"), sem("z_done")
        xp_made, xp_copied, bc_split = sem("xp_made"), sem("xp_copied"), sem("bc_split")
        d_made, d_read, soft = sem("d_made"), sem("d_read"), sem("soft")
        w1_made, dt_ops, dtu_made = sem("w1_made"), sem("dt_ops"), sem("dtu_made")
        bc_made, bc_copied = sem("bc_made"), sem("bc_copied")
        da_made, dbu_made, scanned, carried = sem("da_made"), sem("dbu_made"), sem("scanned"), sem("carried")
        hc_made, summed, skipped = sem("hc_made"), sem("summed"), sem("skipped")
        gated, o_made, o_read = sem("gated"), sem("o_made"), sem("o_read")
        ln_ops, pow_made, x1_made, xn_made = sem("ln_ops"), sem("pow_made"), sem("x1_made"), sem("xn_made")
        t_made, t_copied, l_made, l_read = sem("t_made"), sem("t_copied"), sem("l_made"), sem("l_read")
        lt_made, lt_copied, sm_ops, ex_made, probs_made = (
            sem("lt_made"), sem("lt_copied"), sem("sm_ops"), sem("ex_made"), sem("probs_made"))
        toggled, stats_seen = sem("toggled"), sem("stats_seen")

        chunk_rows = lambda t, c: t.rearrange("(c q p) d -> c p q d", q=Q, p=P)[c.value()]
        NW = 13

        def chunks(eng, body):
            with eng.Fori(0, NCH // 2) as i:
                for par in range(2):
                    body(Count(i, 2, par), par)

        block = ctx.enter_context(nc.Block())

        @block.sync
        def _(sp):
            def load_xT(f):
                sp.dma_start(xT[:], d["xT"][f.value()]).then_inc(xT_in, 16)

            def load_xk(c):
                sp.dma_start(xk[:], chunk_rows(d["x"], c)).then_inc(xk_in, 16)

            load_xT(Count(None, 0, 0))
            for dst, src in (
                (w_in[:], d["W_in"].rearrange("(k p) n -> p k n", p=P)),
                (w_x[:], d["W_x"].rearrange("(k p) n -> p k n", p=P)),
                (w_dt[DP:DP + R, :], d["W_dt"]),
                (w_out[:], d["W_out"].rearrange("(k p) n -> p k n", p=P)),
                (w_r[:], d["W_r"].rearrange("(k p) n -> p k n", p=P)),
                (conv_w[:], d["conv_w"].rearrange("(m p) k -> p m k", p=P)),
                (conv_b[:], d["conv_b"]), (b_dt[:], d["b_dt"]), (d_par[:], d["D_param"]),
                (a_neg[:], d["A_log"].rearrange("(m p) n -> p m n", p=P)),
                (ident[:], d["ident"]), (pick[:], d["pick"]),
                (nw_row[:], d["nw_rows"]),
            ):
                sp.dma_start(dst, src).then_inc(weights_in, 16)
            sp.dma_start(rb_row[:], d["rb_rows"]).then_inc(weights_in, 16)
            load_xk(Count(None, 0, 0))
            sp.wait_ge(z_made, M)
            load_xT(Count(None, 0, 1))

            def zero_acc(c):
                sp.dma_start(chunk_rows(d["acc"], c),
                             zeros[:].unsqueeze(1).to_broadcast([P, Q, D + 1])).then_inc(zeroed, 16)

            def store(c):
                wait(sp, x1_made, c * 1 + 1)
                sp.dma_start(chunk_rows(d["x1"], c), x1[:]).then_inc(stored, 16)
                wait(sp, lt_copied, c * 1 + 2)
                sp.dma_start(d["logits"].rearrange("e (c q p) -> c q e p", q=Q, p=P)[c.value()],
                             lgT[:]).then_inc(stored, 16)
                wait(sp, probs_made, c * 1 + 1)
                sp.dma_start(chunk_rows(d["table"], c), row[:]).then_inc(stored, 16)

            sp.wait_ge(set_up, 1)

            def body(c, par):
                wait(sp, z_made, c * M + 2 * M)
                load_xT(c + 2)
                zero_acc(c)
                store(c)
                load_xk(c + 1)
                wait(sp, stored, c * 48 + 48)
                sp.sem_inc(store_free, 1)

            chunks(sp, body)
            last = Count(None, 0, NCH)
            zero_acc(last)
            store(last)
            sp.wait_ge(stored, 48 * (NCH + 1))
            sp.wait_ge(zeroed, 16 * (NCH + 1))

        @block.tensor
        def _(pe):
            free = {}

            def bank(b):
                for s, v in free.get(b, ()):
                    wait(pe, s, v)
                return f_ps[:, b, :]

            def project_u(f, ms):
                wait(pe, xT_in, f * 16 + 16)
                for m in ms:
                    out = bank(m % 2)
                    for k in range(KD):
                        mm = pe.matmul(out, w_in[:, k, m * P:(m + 1) * P], xT[:, k, :], start=k == 0, stop=k == KD - 1)
                    mm.then_inc(u_made, 1)
                    free[m % 2] = [(u_copied, f * M + m + 1)]

            def project_z(f, ms):
                for m in ms:
                    out = bank(m % 2)
                    for k in range(KD):
                        mm = pe.matmul(out, w_in[:, k, DI + m * P:DI + (m + 1) * P], xT[:, k, :],
                                       start=k == 0, stop=k == KD - 1)
                    mm.then_inc(z_made, 1)
                    free[m % 2] = [(z_done, f * M + m + 1)]

            def project_x(f):
                wait(pe, uc_made, f * 1 + 1)
                out = bank(0)
                for m in range(M):
                    mm = pe.matmul(out[0:DP + R], w_x[:, m, :], uc[:, m, :], start=m == 0, stop=m == M - 1)
                mm.then_inc(xp_made, 1)
                free[0] = [(bc_split, f * 4 + 1), (xp_copied, f * 2 + 2)]

            def project_dt(f, ms):
                wait(pe, xp_copied, f * 2 + 2)
                for m in ms:
                    b = (m + 1) % 2
                    out = bank(b)
                    pe.matmul(out, w_dt[DP:DP + R, m * P:(m + 1) * P], dt_r[DP:DP + R, :],
                              start=True, stop=True).then_inc(d_made, 1)
                    free[b] = [(d_read, f * M + m + 1)]

            def spread(c, n, par):
                if n == 0:
                    wait(pe, bc_split, c * 4 + 4)
                for j in range(2):
                    wait(pe, bc_copied, c * 2 * N + 2 * n + 1 + j)
                    pe.matmul(bc_ps[:, j, :], pick[:, j * N + n, :], bc[:, par, :],
                              start=True, stop=True).then_inc(bc_made, 1)

            def skip(c):
                wait(pe, gated, c * 1 + 1)
                for m in range(M):
                    mm = pe.matmul(y_ps[:, m, :], d_diag[:, m, :], uc[:, m, :], start=True, stop=False)
                mm.then_inc(skipped, 1)

            def add_state(c, n, par):
                wait(pe, hc_made, c * N + n + 5)
                for m in range(M):
                    mm = pe.matmul(y_ps[:, m, :], ident[:], hc[:, n % 2, m, :], start=False, stop=n == N - 1)
                mm.then_inc(summed, 1)

            def output(c):
                wait(pe, gated, c * 1 + 1)
                for q in range(Q):
                    if q % 2 == 0:
                        out = bank(q // 2)
                    for m in range(M):
                        mm = pe.matmul(out[:, (q % 2) * D:(q % 2 + 1) * D], work[:, m, q * P:(q + 1) * P],
                                       w_out[:, m, :], start=m == 0, stop=m == M - 1)
                    if q % 2:
                        mm.then_inc(o_made, 1)
                        free[q // 2] = [(o_read, c * 2 + q // 2 + 1)]

            def turn_xn(c):
                wait(pe, xn_made, c * 1 + 1)
                for k in range(KD):
                    b = 1 - k
                    out = bank(b)
                    for q in range(Q):
                        mm = pe.transpose(out[:, q * P:(q + 1) * P], row[:, q, k * P:(k + 1) * P], ident[:])
                    mm.then_inc(t_made, 1)
                    free[b] = [(t_copied, c * 2 + k + 1)]

            def route(c):
                wait(pe, t_copied, c * 2 + 2)
                out = bank(1)
                for q in range(Q):
                    for k in range(KD):
                        mm = pe.matmul(out[:, q * E:(q + 1) * E], xnT[:, k, q * P:(q + 1) * P], w_r[:, k, :],
                                       start=k == 0, stop=k == KD - 1)
                mm.then_inc(l_made, 1)
                free[1] = [(l_read, c * 1 + 2)]

            def turn_logits(c):
                wait(pe, l_read, c * 1 + 2)
                out = bank(0)
                pe.transpose(out[:, 0:P], lg_wide[:], ident[:]).then_inc(lt_made, 1)
                free[0] = [(lt_copied, c * 1 + 2)]

            pe.wait_ge(weights_in, 16 * (NW + 1))
            first = Count(None, 0, 0)
            project_u(first, range(M))
            project_z(first, range(M))
            project_x(first)
            project_dt(first, range(M))
            pe.wait_ge(set_up, 3)
            for n in range(3):
                spread(first, n, 0)

            def body(c, par):
                f = c + 1
                free[0] = [(lt_copied, c * 1 + 1), (d_read, c * M + M)]
                free[1] = [(l_read, c * 1 + 1), (d_read, c * M + M)]
                for n in range(N):
                    s = n + 3
                    spread(c if s < N else f, s % N, par if s < N else 1 - par)
                    if n == 0:
                        project_u(f, (0, 1))
                        skip(c)
                    if n == 1:
                        project_u(f, (2, 3))
                    if n == 2:
                        output(c)
                    if n == 4:
                        project_z(f, (0, 1))
                    if n == 6:
                        project_z(f, (2, 3))
                    if n == 7:
                        project_x(f)
                    if n == 8:
                        project_dt(f, (0, 1))
                    if n == 9:
                        project_dt(f, (2, 3))
                        turn_xn(c)
                    if n == 10:
                        route(c)
                    if n == 11:
                        turn_logits(c)
                    add_state(c, n, par)

            chunks(pe, body)
            last = Count(None, 0, NCH)
            free.clear()
            output(last)
            turn_xn(last)
            route(last)
            turn_logits(last)

        @block.scalar
        def _(act):
            def copy_u(f, ms):
                if f.per or f.base:
                    wait(act, dt_ops, f * 3)
                for m in ms:
                    wait(act, u_made, f * M + m + 1)
                    act.activation(u[:, m, TAPS - 1:], f_ps[:, m % 2, :], ACT.Copy).then_inc(u_copied, 1)

            def silus(f, par):
                if f.per or f.base:
                    wait(act, skipped, f * 1)
                    wait(act, dtu_made, f * 1)
                wait(act, conv_ops, f * 16 + 16)
                act.activation(uc[:], work[:], ACT.Silu).then_inc(uc_made, 1)
                if f.per or f.base:
                    wait(act, gated, f * 1)
                for m in range(M):
                    wait(act, z_made, f * M + m + 1)
                    act.activation(sz[:, par, m, :], f_ps[:, m % 2, :], ACT.Silu).then_inc(z_done, 1)

            def copy_xp(f, par):
                wait(act, xp_made, f * 1 + 1)
                act.activation(dt_r[DP:DP + R, :], f_ps[DP:DP + R, 0, :], ACT.Copy).then_inc(xp_copied, 1)
                act.activation(bc[:, par, :], f_ps[0:DP, 0, :], ACT.Copy).then_inc(xp_copied, 1)

            def softplus(f, par):
                for m in range(M):
                    wait(act, d_made, f * M + m + 1)
                    src = f_ps[:, (m + 1) % 2, :]
                    act.activation(work[:, m, :], src, ACT.Abs, bias=b_dt[:, m:m + 1])
                    act.activation(dt[:, par, m, :], src, ACT.Relu, bias=b_dt[:, m:m + 1]).then_inc(d_read, 1)
                wait(act, d_read, f * M + M)
                act.activation(work[:], work[:], ACT.Exp, scale=-1.0).then_inc(soft, 1)
                wait(act, soft, f * 2 + 1)
                act.activation(dtu[:, par], work[:], ACT.Ln, bias=1.0).then_inc(soft, 1)

            def copy_bc(c, n):
                wait(act, bc_made, c * 2 * N + 2 * n + 1)
                wait(act, dbu_made, c * N + n + 1)
                act.activation(b_row[:, n % 2, :], bc_ps[:, 0, :], ACT.Copy).then_inc(bc_copied, 1)
                wait(act, bc_made, c * 2 * N + 2 * n + 2)
                wait(act, hc_made, c * N + n + 1)
                act.activation(c_row[:, n % 4, :], bc_ps[:, 1, :], ACT.Copy).then_inc(bc_copied, 1)

            def decay(c, n, par):
                if n == 0:
                    wait(act, dt_ops, c * 3 + 3)
                wait(act, scanned, c * N + n + 1)
                for m in range(M):
                    e = act.activation(da[:, n % 2, m, :], dt[:, par, m, :], ACT.Exp, scale=a_neg[:, m, n:n + 1])
                e.then_inc(da_made, 1)

            def copy_xnT(c):
                for k in range(KD):
                    wait(act, t_made, c * 2 + k + 1)
                    act.activation(xnT[:, k, :], f_ps[:, 1 - k, :], ACT.Copy).then_inc(t_copied, 1)

            def exp_logits(c):
                wait(act, sm_ops, c * 4 + 2)
                act.activation(lg_e[:], lg_d[:], ACT.Exp).then_inc(ex_made, 1)

            def copy_lgT(c):
                wait(act, lt_made, c * 1 + 1)
                wait(act, store_free, c * 1 + 1)
                act.activation(lgT[:], f_ps[0:Q * E, 0, 0:P], ACT.Copy).then_inc(lt_copied, 1)

            act.wait_ge(weights_in, 16 * (NW + 1))
            act.activation(a_neg[:], a_neg[:], ACT.Exp).then_inc(a_ready, 1)
            act.wait_ge(a_ready, 1)
            act.activation(a_neg[:], a_neg[:], ACT.Copy, scale=-1.0).then_inc(a_ready, 1)
            act.wait_ge(a_ready, 2)
            first = Count(None, 0, 0)
            copy_u(first, range(M))
            silus(first, 0)
            copy_xp(first, 0)
            softplus(first, 0)
            copy_bc(first, 0)
            copy_bc(first, 1)
            decay(first, 0, 0)

            def body(c, par):
                f = c + 1
                for n in range(N):
                    s = n + 2
                    copy_bc(c if s < N else f, s % N)
                    s = n + 1
                    decay(c if s < N else f, s % N, par if s < N else 1 - par)
                    if n == 0:
                        copy_u(f, (0, 1))
                    if n == 1:
                        copy_u(f, (2, 3))
                    if n == 6:
                        silus(f, 1 - par)
                    if n == 7:
                        copy_xp(f, 1 - par)
                    if n == 9:
                        softplus(f, 1 - par)
                    if n == 10:
                        copy_xnT(c)
                    if n == 12:
                        exp_logits(c)
                        copy_lgT(c)

            chunks(act, body)
            last = Count(None, 0, NCH)
            copy_xnT(last)
            exp_logits(last)
            copy_lgT(last)

        @block.vector
        def _(dve):
            def put_halo(f):
                if f.per or f.base:
                    wait(dve, dt_ops, f * 3)
                dve.tensor_copy(u[:, :, 0:TAPS - 1], halo[:]).then_inc(halo_put, 1)

            def convolve(f, taps):
                if taps[0] == 0:
                    wait(dve, halo_put, f * 1 + 1)
                    wait(dve, u_copied, f * M + M)
                    if f.per or f.base:
                        wait(dve, o_made, f * 2)
                for j in taps:
                    k = TAPS - 1 - j
                    for m in range(M):
                        if j == 0:
                            op = dve.tensor_scalar(work[:, m, :], u[:, m, k:k + CH], conv_w[:, m, k:k + 1],
                                                   conv_b[:, m:m + 1], ALU.mult, ALU.add)
                        else:
                            wait(dve, conv_ops, f * 16 + 4 * (j - 1) + m + 1)
                            op = dve.scalar_tensor_tensor(work[:, m, :], u[:, m, k:k + CH], conv_w[:, m, k:k + 1],
                                                          work[:, m, :], ALU.mult, ALU.add)
                        op.then_inc(conv_ops, 1)

            def save_halo(f, cut):
                wait(dve, halo_put, f * 1 + 1)
                if cut:
                    dve.tensor_tensor(halo[:].bitcast(I32), u[:, :, CH:].bitcast(I32),
                                      keep[:, 0:M * (TAPS - 1)].rearrange("p (m t) -> p m t", m=M),
                                      ALU.bitwise_and).then_inc(halo_saved, 1)
                else:
                    dve.tensor_copy(halo[:], u[:, :, CH:]).then_inc(halo_saved, 1)

            def split_bc(f, par):
                wait(dve, xp_copied, f * 2 + 2)
                dve.tensor_tensor(bc_rest[:], f_ps[0:DP, 0, :], bc[:, par, :], ALU.subtract).then_inc(bc_split, 1)
                wait(dve, bc_split, f * 4 + 1)
                dve.tensor_copy(bc[32:64, par, :], bc_rest[32:64, :]).then_inc(bc_split, 1)
                dve.tensor_copy(bc_mid[64:96, :], bc_rest[64:96, :]).then_inc(bc_split, 1)
                wait(dve, bc_split, f * 4 + 3)
                dve.tensor_tensor(bc[64:96, par, :], bc_rest[64:96, :], bc_mid[64:96, :],
                                  ALU.subtract).then_inc(bc_split, 1)

            def round_trip(f):
                wait(dve, soft, f * 2 + 1)
                wait(dve, halo_saved, f * 1 + 1)
                dve.tensor_scalar(u[:, :, 0:CH], work[:], 1.0, -1.0, ALU.add, ALU.add).then_inc(w1_made, 1)

            def dt_times_u(f, par):
                wait(dve, dt_ops, f * 3 + 3)
                dve.tensor_tensor(dtu[:, par], dt[:, par], uc[:], ALU.mult).then_inc(dtu_made, 1)

            def drive(c, n, par):
                if n == 0:
                    wait(dve, dtu_made, c * 1 + 1)
                wait(dve, bc_copied, c * 2 * N + 2 * n + 3)
                wait(dve, hc_made, c * N + n + 1)
                wait(dve, carried, c * N + n + 13)
                dve.tensor_tensor(h[:, n % 4], dtu[:, par], b_row[:, n % 2, :].unsqueeze(1).to_broadcast([P, M, CH]),
                                  ALU.mult).then_inc(dbu_made, 1)

            def scan(c, n):
                wait(dve, da_made, c * N + n + 1)
                wait(dve, dbu_made, c * N + n + 3)
                wait(dve, carried, c * N + n + 1)
                for m in range(M):
                    op = dve.tensor_tensor_scan(h[:, n % 4, m, :], da[:, n % 2, m, :], h[:, n % 4, m, :],
                                                state[:, n, m:m + 1], ALU.mult, ALU.add)
                op.then_inc(scanned, 1)

            def carry(c, n, cut):
                wait(dve, scanned, c * N + n + 3)
                last = h[:, n % 4, :, CH - 1:CH]
                out = state[:, n, :].unsqueeze(2)
                if cut:
                    op = dve.tensor_tensor(out.bitcast(I32), last.bitcast(I32), keep[:, 0:M].unsqueeze(2),
                                           ALU.bitwise_and)
                else:
                    op = dve.tensor_copy(out, last)
                op.then_inc(carried, 1)

            def gate(c, par):
                wait(dve, summed, c * N + 2)
                wait(dve, z_done, c * M + M)
                wait(dve, dt_ops, c * 3 + 3)
                dve.tensor_tensor(work[:], y_ps[:], sz[:, 1 - par], ALU.mult).then_inc(gated, 1)

            def normalize(c):
                wait(dve, xk_in, c * 16 + 16)
                for j in range(2):
                    wait(dve, o_made, c * 2 + j + 1)
                    dve.tensor_tensor(xk[:, 2 * j:2 * j + 2, :].rearrange("p q d -> p (q d)"), f_ps[:, j, :],
                                      xk[:, 2 * j:2 * j + 2, :].rearrange("p q d -> p (q d)"),
                                      ALU.add).then_inc(o_read, 1)
                for q in range(Q):
                    wait(dve, o_read, c * 2 + q // 2 + 1)
                    dve.bn_stats(stats[:, q, :], xk[:, q, :]).then_inc(ln_ops, 1)
                wait(dve, ln_ops, c * 12 + Q)
                dve.sem_inc(stats_seen, 1)
                for q in range(Q):
                    dve.bn_aggr(mv[:, q, :], stats[:, q, :]).then_inc(ln_ops, 1)
                wait(dve, ln_ops, c * 12 + 8)
                dve.tensor_scalar(var_e[:, 0, :], mv[:, :, 1], EPS, None, ALU.add).then_inc(ln_ops, 1)
                wait(dve, ln_ops, c * 12 + 9)
                dve.reciprocal(rvar[:], var_e[:, 0, :]).then_inc(ln_ops, 1)
                wait(dve, ln_ops, c * 12 + 10)
                dve.tensor_tensor(rms[:], rvar[:], mv[:, :, 1], ALU.mult).then_inc(ln_ops, 1)
                wait(dve, ln_ops, c * 12 + 11)
                dve.tensor_scalar(var_e[:, 1, :], rms[:], EPS, None, ALU.add).then_inc(ln_ops, 1)

            def scale_rows(c):
                wait(dve, pow_made, c * 1 + 1)
                wait(dve, store_free, c * 1 + 1)
                for q in range(Q):
                    op = dve.tensor_scalar(x1[:, q, :], xk[:, q, :], mv[:, q, 0:1], scales[:, 0, q:q + 1],
                                           ALU.subtract, ALU.mult)
                op.then_inc(x1_made, 1)
                wait(dve, x1_made, c * 1 + 1)
                for q in range(Q):
                    op = dve.scalar_tensor_tensor(row[:, q, 0:D], x1[:, q, :], scales[:, 1, q:q + 1], nw_row[:],
                                                  ALU.mult, ALU.mult)
                op.then_inc(xn_made, 1)

            def logits(c):
                wait(dve, l_made, c * 1 + 1)
                dve.tensor_tensor(lg, f_ps[:, 1, 0:Q * E].rearrange("p (q e) -> p q e", q=Q),
                                  rb_row[:].unsqueeze(1).to_broadcast([P, Q, E]), ALU.add).then_inc(l_read, 1)
                wait(dve, l_read, c * 1 + 2)
                dve.tensor_reduce(lg_max[:], lg, AX.X, ALU.max).then_inc(sm_ops, 1)
                wait(dve, sm_ops, c * 4 + 1)
                dve.tensor_tensor(lg_d[:], lg, lg_max[:].unsqueeze(2).to_broadcast([P, Q, E]),
                                  ALU.subtract).then_inc(sm_ops, 1)

            def softmax(c):
                wait(dve, ex_made, c * 1 + 1)
                dve.tensor_reduce(lg_s[:], lg_e[:], AX.X, ALU.add).then_inc(sm_ops, 1)
                wait(dve, sm_ops, c * 4 + 3)
                dve.reciprocal(lg_r[:], lg_s[:]).then_inc(sm_ops, 1)
                wait(dve, sm_ops, c * 4 + 4)
                dve.tensor_tensor(row[:, :, D:], lg_e[:], lg_r[:].unsqueeze(2).to_broadcast([P, Q, E]),
                                  ALU.mult).then_inc(probs_made, 1)

            dve.memset(zeros[:], 0.0).then_inc(set_up, 1)
            dve.memset(neg_half[:], -0.5)
            dve.memset(halo[:], 0.0)
            dve.memset(lg_wide[:], 0.0)
            dve.memset(state[:], 0.0)
            dve.memset(keep[:], -1)
            dve.memset(sz[:, 1], 0.0)
            dve.memset(y_ps[:], 0.0).then_inc(set_up, 1)
            dve.wait_ge(weights_in, 16 * (NW + 1))
            for m in range(M):
                op = dve.tensor_scalar(d_diag[:, m, :], ident[:], d_par[:, m:m + 1], None, ALU.mult)
            op.then_inc(set_up, 1)
            dve.wait_ge(set_up, 3)
            dve.sem_inc(dbu_made, 2)
            dve.sem_inc(scanned, 2)
            dve.sem_inc(carried, N)
            dve.sem_inc(l_read, 1)
            dve.sem_inc(bc_copied, 2)
            dve.sem_inc(hc_made, 4)
            dve.sem_inc(summed, 2)
            dve.sem_inc(lt_copied, 1)
            dve.sem_inc(store_free, 1)
            first = Count(None, 0, 0)
            put_halo(first)
            convolve(first, range(TAPS))
            save_halo(first, False)
            split_bc(first, 0)
            round_trip(first)
            dt_times_u(first, 0)

            def body(c, par):
                f = c + 1
                drive(c, 0, par)
                for n in range(N):
                    if n + 1 < N:
                        drive(c, n + 1, par)
                    if n:
                        carry(c, n - 1, par == 1)
                    scan(c, n)
                    if n == 1:
                        gate(c, par)
                        put_halo(f)
                    if n == 3:
                        normalize(c)
                        convolve(f, (0,))
                    if n == 4:
                        convolve(f, (1, 2))
                    if n == 5:
                        convolve(f, (3,))
                        save_halo(f, par == 0)
                    if n == 6:
                        scale_rows(c)
                    if n == 8:
                        split_bc(f, 1 - par)
                    if n == 10:
                        round_trip(f)
                    if n == 11:
                        logits(c)
                    if n == 13:
                        softmax(c)
                dt_times_u(f, 1 - par)
                carry(c, N - 1, par == 1)
                if par == 1:
                    wait(dve, carried, c * N + 2 * N)
                    wait(dve, halo_saved, f * 1 + 1)
                    dve.tensor_scalar(keep[:], keep[:], -1, None, ALU.bitwise_xor).then_inc(toggled, 1)
                    wait(dve, toggled, Count(c.reg, 1, 1))

            chunks(dve, body)
            last = Count(None, 0, NCH)
            gate(last, 0)
            normalize(last)
            scale_rows(last)
            logits(last)
            softmax(last)

        @block.gpsimd
        def _(pool):
            def sum_dt(f, par, j):
                if j == 0:
                    wait(pool, w1_made, f * 1 + 1)
                    wait(pool, soft, f * 2 + 2)
                    op = pool.tensor_tensor(work[:], work[:], u[:, :, 0:CH], ALU.subtract)
                if j == 1:
                    op = pool.tensor_tensor(dt[:, par], dt[:, par], dtu[:, par], ALU.add)
                if j == 2:
                    wait(pool, dt_ops, f * 3 + 2)
                    op = pool.tensor_tensor(dt[:, par], dt[:, par], work[:], ALU.add)
                op.then_inc(dt_ops, 1)

            def times_c(c, n):
                wait(pool, scanned, c * N + n + 3)
                wait(pool, bc_copied, c * 2 * N + 2 * n + 4)
                wait(pool, summed, c * N + n + 1)
                pool.tensor_tensor(hc[:, n % 2], h[:, n % 4], c_row[:, n % 4, :].unsqueeze(1).to_broadcast([P, M, CH]),
                                   ALU.mult).then_inc(hc_made, 1)

            def roots(c):
                wait(pool, ln_ops, c * 12 + 12)
                pool.tensor_tensor(scales[:].rearrange("p a q -> p (a q)"), var_e[:].rearrange("p a q -> p (a q)"),
                                   neg_half[:], ALU.pow).then_inc(pow_made, 1)

            pool.wait_ge(set_up, 3)
            first = Count(None, 0, 0)
            for j in range(3):
                sum_dt(first, 0, j)

            def body(c, par):
                for n in range(N):
                    times_c(c, n)
                    if n == 3:
                        roots(c)
                    if n in (10, 11, 12):
                        sum_dt(c + 1, 1 - par, n - 10)

            chunks(pool, body)
            roots(Count(None, 0, NCH))


def experts_phase(nc, d):
    E = d["logits"].shape[0]
    T = d["logits"].shape[1] - CH
    D = d["x"].shape[1]
    KD = D // P
    F = d["W1"].shape[3]
    FT = F // P
    K = max(1, -(-T // E))
    J = P // E
    TJ = T // J
    NB = TJ // P
    KT = K // P
    HT = min(KT, CH // P)
    HALVES = KT // HT
    HW = HT * P
    NCK = NB * J
    assert K % P == 0 and TJ % P == 0 and NCK + Q <= 256 and KT % HT == 0

    with ExitStack() as ctx:
        def sb(name, shape, dt=F32):
            return ctx.enter_context(nc.sbuf_tensor("sb_" + name, shape, dt))

        def sem(name):
            return ctx.enter_context(nc.semaphore(name))

        slot_lo = sb("slot_lo", [P, NB, P], BF16)
        slot_hi = sb("slot_hi", [P, NB, P], BF16)
        same = sb("same", [P, P])
        before = sb("before", [P, P])
        ident = sb("ident2", [P, P])
        ident_h = sb("ident_h", [P, P], BF16)

        with ExitStack() as ctx2:
            def sb2(name, shape, dt=F32):
                return ctx2.enter_context(nc.sbuf_tensor("sb_" + name, shape, dt))

            def sem2(name):
                return ctx2.enter_context(nc.semaphore(name))

            lg = sb2("lg_all", [P, TJ])
            above = sb2("above", [P, TJ])
            tied = sb2("tied", [P, TJ])
            n_above = sb2("n_above", [P, TJ])
            n_tied = sb2("n_tied", [P, TJ])
            slot_i = sb2("slot_i", [P, TJ], I32)
            part_i = sb2("part_i", [P, 2, TJ], I32)
            part_h = sb2("part_h", [P, 2, TJ], BF16)
            one = sb2("one", [P, 1])
            key, bit, cand, flip, thr = (sb2(n, [P, 1], I32) for n in ("key", "bit", "cand", "flip", "thr"))
            take = sb2("take", [P, 1], I32)
            counts = sb2("counts", [P, 2])
            before_n = sb2("before_n", [P, 2])
            need = sb2("need", [P, 1])
            cnt_ps = ctx2.enter_context(nc.psum_tensor("cnt_ps", [P, CH], F32))
            cut_ps = ctx2.enter_context(nc.psum_tensor("cut_ps", [P, 2, 8 * P], BF16))
            tk_in, tk_set, key_ops, counted, totalled, cut_ops, listed = (
                sem2("tk_in"), sem2("tk_set"), sem2("key_ops"), sem2("counted"), sem2("totalled"),
                sem2("cut_ops"), sem2("listed"))
            cut_made, cut_copied = sem2("cut_made"), sem2("cut_copied")
            OPS = 7
            GRP = min(NB, 8)

            with nc.Block() as block:
                @block.sync
                def _(sp):
                    sp.dma_start(lg[:], d["logits"][:, CH:].rearrange("e (j t) -> e j t", j=J)).then_inc(tk_in, 16)
                    for dst, src in ((same, "same"), (before, "before"), (ident, "ident"), (ident_h, "ident_h")):
                        sp.dma_start(dst[:], d[src]).then_inc(tk_in, 16)

                @block.vector
                def _(dve):
                    def threshold(src, op_no, base):
                        wait(dve, key_ops, base + op_no)
                        dve.tensor_scalar(flip[:], src[:], 31, -1, ALU.arith_shift_right,
                                          ALU.bitwise_xor).then_inc(key_ops, 1)
                        wait(dve, key_ops, base + op_no + 1)
                        dve.scalar_tensor_tensor(thr[:], flip[:], -2 ** 31, src[:], ALU.bitwise_or,
                                                 ALU.bitwise_xor).then_inc(key_ops, 1)

                    dve.memset(key[:], 0)
                    dve.memset(one[:], 1.0)
                    dve.memset(bit[:], -2 ** 31).then_inc(tk_set, 1)
                    dve.wait_ge(tk_set, 1)
                    dve.wait_ge(tk_in, 80)
                    with dve.Fori(0, 32) as r:
                        round_ = Count(r, OPS, 0)
                        wait(dve, tk_set, Count(r, 1, 1))
                        dve.tensor_tensor(cand[:], key[:], bit[:], ALU.bitwise_or).then_inc(key_ops, 1)
                        threshold(cand, 1, round_)
                        wait(dve, key_ops, round_ + 3)
                        dve.tensor_scalar(above[:], lg[:], thr[:].bitcast(F32), 0.0, ALU.is_ge, ALU.add,
                                          accum_out=counts[:, 0:1]).then_inc(counted, 1)
                        wait(dve, totalled, Count(r, 1, 1))
                        dve.tensor_scalar(take[:], cnt_ps[:, 0:1], float(K), -1.0, ALU.is_ge,
                                          ALU.mult).then_inc(key_ops, 1)
                        wait(dve, key_ops, round_ + 4)
                        dve.scalar_tensor_tensor(key[:], take[:], bit[:], key[:], ALU.bitwise_and,
                                                 ALU.bitwise_or).then_inc(key_ops, 1)
                        wait(dve, key_ops, round_ + 5)
                        dve.tensor_scalar(bit[:], bit[:], 1, None, ALU.logical_shift_right).then_inc(key_ops, 1)
                        wait(dve, key_ops, round_ + 6)
                        dve.tensor_scalar(bit[:], bit[:], 2 ** 31 - 1, None, ALU.bitwise_and).then_inc(key_ops, 1)
                        wait(dve, key_ops, round_ + 7)
                        dve.sem_inc(tk_set, 1)

                    threshold(key, 7, Count(None, 0, OPS * 31))
                    done = OPS * 32 + 2
                    dve.wait_ge(key_ops, done)
                    dve.tensor_scalar(above[:], lg[:], thr[:].bitcast(F32), 0.0, ALU.is_gt, ALU.add,
                                      accum_out=counts[:, 0:1])
                    dve.tensor_scalar(tied[:], lg[:], thr[:].bitcast(F32), 0.0, ALU.is_equal, ALU.add,
                                      accum_out=counts[:, 1:2]).then_inc(counted, 1)
                    dve.wait_ge(totalled, 33)
                    dve.tensor_copy(before_n[:], cnt_ps[:, 2:4])
                    dve.tensor_scalar(need[:], cnt_ps[:, 0:1], -1.0, float(K), ALU.mult, ALU.add).then_inc(cut_ops, 1)
                    dve.wait_ge(cut_ops, 1)
                    ones = one[:].to_broadcast([P, TJ])
                    dve.tensor_tensor_scan(n_above[:], ones, above[:], before_n[:, 0:1], ALU.mult, ALU.add)
                    dve.tensor_tensor_scan(n_tied[:], ones, tied[:], before_n[:, 1:2], ALU.mult,
                                           ALU.add).then_inc(cut_ops, 1)
                    dve.wait_ge(cut_ops, 2)
                    dve.scalar_tensor_tensor(tied[:], n_tied[:], need[:], tied[:], ALU.is_le, ALU.mult)
                    dve.scalar_tensor_tensor(n_above[:], n_tied[:], need[:], n_above[:], ALU.min,
                                             ALU.add).then_inc(cut_ops, 1)
                    dve.wait_ge(cut_ops, 3)
                    dve.tensor_tensor(above[:], above[:], tied[:], ALU.add).then_inc(cut_ops, 1)
                    dve.wait_ge(cut_ops, 4)
                    dve.tensor_tensor(above[:], above[:], n_above[:], ALU.mult).then_inc(cut_ops, 1)
                    dve.wait_ge(cut_ops, 5)
                    dve.tensor_scalar(slot_i[:], above[:], float(P - 1), None, ALU.add).then_inc(cut_ops, 1)
                    dve.wait_ge(cut_ops, 6)
                    dve.tensor_scalar(part_i[:, 0], slot_i[:], P - 1, None, ALU.bitwise_and)
                    dve.tensor_scalar(part_i[:, 1], slot_i[:], 7, None, ALU.logical_shift_right).then_inc(cut_ops, 1)
                    dve.wait_ge(cut_ops, 7)
                    dve.tensor_copy(part_h[:], part_i[:]).then_inc(cut_ops, 1)
                    n = 0
                    for dst in (slot_lo, slot_hi):
                        for b in range(0, NB, GRP):
                            n += 1
                            dve.wait_ge(cut_made, n)
                            dve.tensor_copy(dst[:, b:b + GRP, :].rearrange("p b e -> p (b e)"),
                                            cut_ps[:, n % 2, 0:GRP * P]).then_inc(cut_copied, 1)

                @block.tensor
                def _(pe):
                    pe.wait_ge(tk_in, 80)
                    with pe.Fori(0, 32) as r:
                        wait(pe, counted, Count(r, 1, 1))
                        pe.matmul(cnt_ps[:, 0:1], same[:], counts[:, 0:1], start=True, stop=True).then_inc(totalled, 1)
                    pe.wait_ge(counted, 33)
                    pe.matmul(cnt_ps[:, 0:2], same[:], counts[:], start=True, stop=True)
                    pe.matmul(cnt_ps[:, 2:4], before[:], counts[:], start=True, stop=True).then_inc(totalled, 1)
                    pe.wait_ge(cut_ops, 8)
                    n = 0
                    for part in range(2):
                        for b in range(0, NB, GRP):
                            n += 1
                            if n > 2:
                                pe.wait_ge(cut_copied, n - 2)
                            for g in range(GRP):
                                t = pe.transpose(cut_ps[:, n % 2, g * P:(g + 1) * P],
                                                 part_h[:, part, (b + g) * P:(b + g + 1) * P], ident_h[:])
                            t.then_inc(cut_made, 1)

        iota_lo = sb("iota_lo", [P, P, J], BF16)
        iota_hi = sb("iota_hi", [P, KT, J], BF16)
        block_no = sb("block_no", [P, NB, J], BF16)
        part_no = sb("part_no", [P, 1])
        b1 = sb("b1", [P, 2, FT])
        b2 = sb("b2", [P, 2, D])
        w1 = sb("w1", [P, 2, KD, F])
        w2 = sb("w2", [P, 2, FT, D])
        hot_lo = sb("hot_lo", [P, P, NB, J], BF16)
        hot_hi = sb("hot_hi", [P, KT, NB, J], BF16)
        where = sb("where", [P, 2, KT, NB, J], BF16)
        where_f = sb("where_f", [P, KT])
        idx = sb("idx", [P, 2, KT], I32)
        rows = sb("rows", [P, 2, KT, D + E])
        gates = sb("gates", [P, 2, KT])
        xeT = sb("xeT", [P, 2, KD, K])
        hT = sb("hT", [P, FT, K])
        yb = sb("yb", [P, KT, D])
        give = sb("give", [P, 2, KT, D + 1])
        list_ps = ctx.enter_context(nc.psum_tensor("list_ps", [P, CH], F32))[:, 0:2 * KT]
        turn_ps = ctx.enter_context(nc.psum_tensor("turn_ps", [P, 2, HW], F32))
        h_ps = ctx.enter_context(nc.psum_tensor("h_ps", [P, 2, CH], F32))
        o_ps = ctx.enter_context(nc.psum_tensor("o_ps", [P, 2, 2, D], F32))
        ex_in, w_in, hots, list_made, idx_ops, gathered, gates_made = (
            sem("ex_in"), (sem("even_w_in"), sem("odd_w_in")), sem("hots"), sem("list_made"), sem("idx_ops"), sem("gathered"),
            sem("gates_made"))
        turned, turn_copied, fc1_made, gelu_made, fc2_made, bias_added, given, added, waited = (
            sem("turned"), sem("turn_copied"), sem("fc1_made"), sem("gelu_made"), sem("fc2_made"),
            sem("bias_added"), sem("given"), sem("added"), sem("waited"))
        PAIRS = -(-KT // 2)
        TURNS = HALVES * KD

        def pair_no(e, par):
            return Count(e.reg, e.per // 2, (e.base - par) // 2 + 1)

        def experts(eng, body):
            for par in range(2):
                body(Count(None, 0, par), par, False)
            with eng.Fori(0, E // 2 - 2) as i:
                for par in range(2):
                    body(Count(i, 2, par + 2), par, False)
            for par in range(2):
                body(Count(None, 0, E - 2 + par), par, par == 1)

        NC2 = 4
        with nc.Block() as block:
            @block.sync
            def _(sp):
                def load(e, par):
                    for dst, src in ((w1, "W1"), (b1, "b1"), (w2, "W2"), (b2, "b2_rows")):
                        sp.dma_start(dst[:, par], d[src][e.value()]).then_inc(w_in[par], 16)

                for dst, src in ((iota_lo, "iota_lo"), (iota_hi, "iota_hi"), (block_no, "block_no"),
                                 (part_no, "part_no")):
                    sp.dma_start(dst[:], d[src]).then_inc(ex_in, 16)
                load(Count(None, 0, 0), 0)
                load(Count(None, 0, 1), 1)

                def body(e, par, last):
                    if e.per or e.base < E - 2:
                        wait(sp, bias_added, (e + 1) * PAIRS)
                        load(e + 2, par)

                experts(sp, body)

            @block.tensor
            def _(pe):
                def make_list(e):
                    wait(pe, hots, (e + 1) * 4)
                    if e.per or e.base:
                        wait(pe, idx_ops, e * 2)
                    for ck in range(NCK):
                        mm = pe.matmul(list_ps, hot_lo[:].rearrange("p i b j -> p i (b j)")[:, :, ck],
                                       where[:].rearrange("p a i b j -> p (a i) (b j)")[:, :, ck],
                                       start=ck == 0, stop=ck == NCK - 1)
                    mm.then_inc(list_made, 1)

                def turn(e, par):
                    wait(pe, gathered, (e + 1) * (16 * KT))
                    for n in range(TURNS):
                        hf, k = divmod(n, KD)
                        if e.per or e.base or n >= 2:
                            wait(pe, turn_copied, e * TURNS + (n - 1))
                        for q in range(HT):
                            t = pe.transpose(turn_ps[:, n % 2, q * P:(q + 1) * P],
                                             rows[:, par, hf * HT + q, k * P:(k + 1) * P], ident[:])
                        t.then_inc(turned, 1)

                def fc1(e, par):
                    wait(pe, w_in[par], pair_no(e, par) * 64)
                    for hf in range(HALVES):
                        wait(pe, turn_copied, e * TURNS + (hf + 1) * KD)
                        for f in range(FT):
                            n = hf * FT + f
                            if e.per or e.base or n >= 2:
                                wait(pe, gelu_made, e * (HALVES * FT) + (n - 1))
                            for k in range(KD):
                                mm = pe.matmul(h_ps[:, n % 2, 0:HW], w1[:, par, k, f * P:(f + 1) * P],
                                               xeT[:, par, k, hf * HW:(hf + 1) * HW], start=k == 0, stop=k == KD - 1)
                            mm.then_inc(fc1_made, 1)

                def fc2(e, par):
                    for q in range(KT):
                        if q % HT == 0:
                            wait(pe, gelu_made, e * (HALVES * FT) + (q // HT + 1) * FT)
                        n = q // 2
                        if q % 2 == 0 and (e.per or e.base or n >= 2):
                            wait(pe, bias_added, e * PAIRS + (n - 1))
                        for f in range(FT):
                            mm = pe.matmul(o_ps[:, n % 2, q % 2, :], hT[:, f, q * P:(q + 1) * P], w2[:, par, f, :],
                                           start=f == 0, stop=f == FT - 1)
                        if q % 2 or q == KT - 1:
                            mm.then_inc(fc2_made, 1)

                first = Count(None, 0, 0)
                make_list(first)
                turn(first, 0)

                def body(e, par, last):
                    fc1(e, par)
                    if not last:
                        make_list(e + 1)
                    fc2(e, par)
                    if not last:
                        turn(e + 1, 1 - par)

                experts(pe, body)

            @block.scalar
            def _(act):
                def copy_turn(e, par):
                    if e.per or e.base > 1:
                        wait(act, fc1_made, (e + -1) * (HALVES * FT))
                    for n in range(TURNS):
                        hf, k = divmod(n, KD)
                        wait(act, turned, e * TURNS + (n + 1))
                        act.activation(xeT[:, par, k, hf * HW:(hf + 1) * HW], turn_ps[:, n % 2, :],
                                       ACT.Copy).then_inc(turn_copied, 1)

                def gelu(e, par):
                    if e.per or e.base:
                        wait(act, fc2_made, e * PAIRS)
                    for hf in range(HALVES):
                        for f in range(FT):
                            n = hf * FT + f
                            wait(act, fc1_made, e * (HALVES * FT) + (n + 1))
                            act.activation(hT[:, f, hf * HW:(hf + 1) * HW], h_ps[:, n % 2, 0:HW], ACT.Gelu,
                                           bias=b1[:, par, f:f + 1]).then_inc(gelu_made, 1)

                def times_gate(e, par):
                    wait(act, gates_made, (e + 1) * 1)
                    if e.per or e.base > 1:
                        wait(act, added, (e + -1) * (16 * KT))
                    for n in range(PAIRS):
                        wait(act, bias_added, e * PAIRS + (n + 1))
                        for q in range(2 * n, min(2 * n + 2, KT)):
                            op = act.activation(give[:, par, q, 0:D], yb[:, q, :], ACT.Copy,
                                                scale=gates[:, par, q:q + 1])
                        op.then_inc(given, 1)

                first = Count(None, 0, 0)
                act.wait_ge(ex_in, 16 * NC2)
                copy_turn(first, 0)

                def body(e, par, last):
                    gelu(e, par)
                    times_gate(e, par)
                    if not last:
                        copy_turn(e + 1, 1 - par)

                experts(act, body)

            @block.vector
            def _(dve):
                def make_hots(e):
                    if e.per or e.base:
                        wait(dve, list_made, e * 1)
                    lo = slot_lo[:].rearrange("p b (e j) -> p e b j", e=E)[:, e.value()]
                    hi = slot_hi[:].rearrange("p b (e j) -> p e b j", e=E)[:, e.value()]
                    dve.tensor_tensor(hot_hi[:], hi.unsqueeze(1).to_broadcast([P, KT, NB, J]),
                                      iota_hi[:].unsqueeze(2).to_broadcast([P, KT, NB, J]),
                                      ALU.is_equal).then_inc(hots, 1)
                    dve.tensor_tensor(hot_lo[:], lo.unsqueeze(1).to_broadcast([P, P, NB, J]),
                                      iota_lo[:].unsqueeze(2).to_broadcast([P, P, NB, J]),
                                      ALU.is_equal).then_inc(hots, 1)
                    wait(dve, hots, e * 4 + 1)
                    dve.tensor_scalar(where[:, 0], hot_hi[:], part_no[:], None, ALU.mult).then_inc(hots, 1)
                    dve.tensor_tensor(where[:, 1], hot_hi[:], block_no[:].unsqueeze(1).to_broadcast([P, KT, NB, J]),
                                      ALU.mult).then_inc(hots, 1)

                def make_idx(e, par):
                    wait(dve, list_made, e * 1 + 1)
                    if e.per or e.base > 1:
                        wait(dve, added, (e + -1) * (16 * KT))
                    dve.tensor_copy(where_f[:], list_ps[:, 0:KT]).then_inc(idx_ops, 1)
                    wait(dve, idx_ops, e * 2 + 1)
                    dve.scalar_tensor_tensor(idx[:, par, :], list_ps[:, KT:], float(P), where_f[:], ALU.mult,
                                             ALU.add).then_inc(idx_ops, 1)

                def copy_gates(e, par):
                    wait(dve, gathered, (e + 1) * (16 * KT))
                    if e.per or e.base > 1:
                        wait(dve, added, (e + -1) * (16 * KT))
                        wait(dve, given, (e + -1) * PAIRS)
                    col = rows[:, par].rearrange("p k d -> p d k")[:, D:, :][:, e.value(), :]
                    dve.tensor_copy(gates[:, par, :], col)
                    dve.tensor_copy(give[:, par, :, D], col).then_inc(gates_made, 1)

                def add_bias(e, par):
                    if e.per or e.base:
                        wait(dve, given, e * PAIRS)
                    for n in range(PAIRS):
                        w = min(2, KT - 2 * n)
                        wait(dve, fc2_made, e * PAIRS + (n + 1))
                        dve.tensor_tensor(yb[:, 2 * n:2 * n + w, :], o_ps[:, n % 2, 0:w, :],
                                          b2[:, par, :].unsqueeze(1).to_broadcast([P, w, D]),
                                          ALU.add).then_inc(bias_added, 1)

                dve.wait_ge(ex_in, 16 * NC2)
                first = Count(None, 0, 0)
                make_hots(first)
                make_idx(first, 0)

                def body(e, par, last):
                    copy_gates(e, par)
                    if not last:
                        make_hots(e + 1)
                        make_idx(e + 1, 1 - par)
                    add_bias(e, par)

                experts(dve, body)

            @block.gpsimd
            def _(pool):
                def gather(e, par):
                    wait(pool, idx_ops, (e + 1) * 2)
                    if e.per or e.base > 1:
                        wait(pool, turned, (e + -1) * TURNS)
                        wait(pool, gates_made, (e + -1) * 1)
                    pool.sem_inc(waited, 1)
                    for q in range(KT):
                        pool.indirect_dma_start(
                            out=rows[:, par, q, :], out_offset=None, in_=d["table"],
                            in_offset=bass.IndirectOffsetOnAxis(ap=idx[:, par, q:q + 1], axis=0)).then_inc(gathered, 16)

                def scatter(e, par):
                    if e.per or e.base:
                        wait(pool, added, e * (16 * KT))
                    wait(pool, given, (e + 1) * PAIRS)
                    pool.sem_inc(waited, 1)
                    for q in range(KT):
                        pool.indirect_dma_start(
                            out=d["acc"], out_offset=bass.IndirectOffsetOnAxis(ap=idx[:, par, q:q + 1], axis=0),
                            in_=give[:, par, q, :], in_offset=None,
                            compute_op=ALU.add).then_inc(added, 16)

                gather(Count(None, 0, 0), 0)

                def body(e, par, last):
                    if not last:
                        gather(e + 1, 1 - par)
                    scatter(e, par)

                experts(pool, body)
                pool.wait_ge(added, E * 16 * KT)


def final_phase(nc, d):
    T, D = d["out"].shape
    R = 4
    NI = T // CH // R

    with ExitStack() as ctx:
        def sb(name, shape, dt=F32):
            return ctx.enter_context(nc.sbuf_tensor("sb_" + name, shape, dt))

        def sem(name):
            return ctx.enter_context(nc.semaphore(name))

        acc = sb("acc_f", [P, R, Q, D + 1])
        x1 = sb("x1_f", [P, R, Q, D])
        out = sb("out_f", [P, R, Q, D])
        none = sb("none_f", [P, R, Q])
        gate_r = sb("gate_r", [P, R, Q])
        stats = sb("stats_f", [P, R, Q, 6])
        mv = sb("mv_f", [P, R, Q, 2])
        var_e = sb("var_e_f", [P, R, Q])
        rstd = sb("rstd_f", [P, R, Q])
        shift = sb("shift_f", [P, R, Q])
        neg_half = sb("neg_half_f", [P, Q])
        loaded = [sem(f"loaded_{r}") for r in range(R)]
        left = [sem(f"left_{r}") for r in range(R)]
        half_set, combine_ops, combined, stats_ops, stats_seen, rooted, shifts, shifted, normed = (
            sem("half_set"), sem("combine_ops"), sem("combined"), sem("stats_ops"), sem("stats_seen_f"), sem("rooted"),
            sem("shifts"), sem("shifted"), sem("normed"))

        def rounds(eng, body):
            body(None)
            with eng.Fori(0, NI - 1) as i:
                body(i)

        def number(i, r):
            return Count(None, 0, r) if i is None else Count(i, R, R + r)

        def turn(i):
            return Count(None, 0, 0) if i is None else Count(i, 1, 1)

        def rows_of(t, c):
            return t.rearrange("(c q p) d -> c p q d", q=Q, p=P)[c.value()]

        with nc.Block() as block:
            @block.sync
            def _(sp):
                def load(c, r):
                    sp.dma_start(acc[:, r], rows_of(d["acc"], c + 1)).then_inc(loaded[r], 16)
                    sp.dma_start(x1[:, r], rows_of(d["x1"], c + 1)).then_inc(loaded[r], 16)

                for r in range(R):
                    load(Count(None, 0, r), r)

                with sp.Fori(0, NI - 1) as i:
                    for r in range(R):
                        wait(sp, normed, Count(i, R, r + 1))
                        load(Count(i, R, R + r), r)

            @block.vector
            def _(dve):
                def combine(i, r):
                    c = number(i, r)
                    wait(dve, loaded[r], turn(i) * 32 + 32)
                    dve.tensor_scalar(none[:, r], acc[:, r, :, D], 0.0, None, ALU.is_le).then_inc(combine_ops, 1)
                    wait(dve, combine_ops, c * 3 + 1)
                    dve.tensor_tensor(none[:, r], acc[:, r, :, D], none[:, r], ALU.add).then_inc(combine_ops, 1)
                    wait(dve, combine_ops, c * 3 + 2)
                    dve.reciprocal(gate_r[:, r], none[:, r]).then_inc(combine_ops, 1)
                    wait(dve, combine_ops, c * 3 + 3)
                    for q in range(Q):
                        dve.scalar_tensor_tensor(x1[:, r, q, :], acc[:, r, q, 0:D], gate_r[:, r, q:q + 1],
                                                 x1[:, r, q, :], ALU.mult, ALU.add).then_inc(combined, 1)
                    for q in range(Q):
                        wait(dve, combined, c * Q + (q + 1))
                        dve.bn_stats(stats[:, r, q, :], x1[:, r, q, :]).then_inc(stats_ops, 1)
                    wait(dve, stats_ops, c * 6 + Q)
                    dve.sem_inc(stats_seen, 1)
                    for q in range(Q):
                        op = dve.bn_aggr(mv[:, r, q, :], stats[:, r, q, :])
                    op.then_inc(stats_ops, 1)
                    wait(dve, stats_ops, c * 6 + 5)
                    dve.tensor_scalar(var_e[:, r], mv[:, r, :, 1], EPS, None, ALU.add).then_inc(stats_ops, 1)

                def shift_of(i, r):
                    c = number(i, r)
                    wait(dve, rooted, c + 1)
                    dve.scalar_tensor_tensor(shift[:, r], mv[:, r, :, 0], -1.0, rstd[:, r], ALU.mult,
                                             ALU.mult).then_inc(shifted, 1)

                dve.memset(neg_half[:], -0.5).then_inc(half_set, 1)

                def body(i):
                    for r in range(R + 1):
                        if r < R:
                            combine(i, r)
                        if r:
                            shift_of(i, r - 1)

                rounds(dve, body)

            @block.gpsimd
            def _(pool):
                pool.wait_ge(half_set, 1)

                def body(i):
                    for r in range(R):
                        wait(pool, stats_ops, number(i, r) * 6 + 6)
                        pool.tensor_tensor(rstd[:, r], var_e[:, r], neg_half[:], ALU.pow).then_inc(rooted, 1)

                rounds(pool, body)

            @block.scalar
            def _(act):
                def body(i):
                    for r in range(R):
                        c = number(i, r)
                        wait(act, shifted, c + 1)
                        if i is not None:
                            wait(act, left[r], turn(i) * 16)
                        for q in range(Q):
                            op = act.activation(out[:, r, q, :], x1[:, r, q, :], ACT.Identity,
                                                scale=rstd[:, r, q:q + 1], bias=shift[:, r, q:q + 1])
                        op.then_inc(normed, 1)
                        wait(act, normed, c + 1)
                        act.dma_start(rows_of(d["out"], c), out[:, r]).then_inc(left[r], 16)

                rounds(act, body)
                for r in range(R):
                    act.wait_ge(left[r], 16 * NI)


def host_layout(inputs):
    half = mybir.dt.np(BF16)
    g = {k.split("_", 2)[2]: np.ascontiguousarray(np.asarray(v)) for k, v in inputs.items()}
    x = g["x"]
    B, L, D = x.shape
    T = B * L
    DI, N = g["A_log"].shape
    R = g["W_dt"].shape[0]
    x = x.reshape(T, D)
    a = {}
    a["x"] = np.concatenate([np.zeros((CH, D), np.float32), x])
    xT = np.zeros((T // CH + 2, P, D // P, CH), np.float32)
    xT[:T // CH] = x.reshape(T // CH, CH, D // P, P).transpose(0, 3, 2, 1)
    a["xT"] = xT
    a["W_in"], a["W_dt"], a["W_out"] = g["W_in"], g["W_dt"], g["W_out"]
    a["W_x"] = np.concatenate([g["W_x"][:, R:]] * 3 + [g["W_x"][:, :R]], axis=1)
    a["W_r"] = np.ascontiguousarray(g["router_weight"].T)
    a["conv_w"], a["A_log"] = g["conv_w"], g["A_log"]
    for n in ("conv_b", "b_dt", "D_param"):
        a[n] = np.ascontiguousarray(g[n].reshape(DI // P, P).T)
    a["ident"] = np.eye(P, dtype=np.float32)
    pick = np.zeros((DP, 2 * N, P), half)
    for n in range(2 * N):
        pick[n::2 * N, n, :] = 1
    a["pick"] = pick
    a["nw_rows"] = np.ascontiguousarray(np.broadcast_to(g["norm_weight"], (P, D)))
    a["rb_rows"] = np.ascontiguousarray(np.broadcast_to(g["router_bias"], (P, len(g["router_bias"]))))
    a["router_bias"] = g["router_bias"]
    E = len(g["router_bias"])
    F = g["fc1_bias"].shape[1]
    J = P // E
    KT = max(1, -(-T // E)) // P
    NB = T // J // P
    part = np.arange(P)
    same = part[:, None] // J == part[None, :] // J
    a["same"] = same.astype(np.float32)
    a["before"] = (same & (part[:, None] < part[None, :])).astype(np.float32)
    a["ident_h"] = np.eye(P, dtype=half)
    bf = lambda v, shape: np.ascontiguousarray(np.broadcast_to(v, shape)).astype(half)
    a["iota_lo"] = bf(np.arange(P)[None, :, None], (P, P, J))
    a["iota_hi"] = bf(np.arange(1, KT + 1)[None, :, None], (P, KT, J))
    a["block_no"] = bf(np.arange(NB)[None, :, None] + np.arange(J)[None, None, :] * NB + Q, (P, NB, J))
    a["part_no"] = np.arange(P, dtype=np.float32)[:, None].copy()
    a["W1"] = np.ascontiguousarray(g["fc1_weight"].reshape(E, F, D // P, P).transpose(0, 3, 2, 1))
    a["W2"] = np.ascontiguousarray(g["fc2_weight"].reshape(E, D, F // P, P).transpose(0, 3, 2, 1))
    a["b1"] = np.ascontiguousarray(g["fc1_bias"].reshape(E, F // P, P).transpose(0, 2, 1))
    a["b2_rows"] = np.ascontiguousarray(np.broadcast_to(g["fc2_bias"][:, None, :], (E, P, D)))
    return a, (B, L, D)


def build(nc, d, T, D, E):
    for name, width in (("x1", D), ("table", D + E), ("acc", D + 1)):
        d[name] = nc.dram_tensor("rows_" + name, (T + CH, width), F32, kind="Internal").ap()
    d["logits"] = nc.dram_tensor("router_logits", (E, T + CH), F32, kind="Internal").ap()
    mamba_phase(nc, d)
    experts_phase(nc, d)
    final_phase(nc, d)


def kernel(**inputs):
    import concourse.bacc as bacc
    from concourse.bass_utils import run_bass_kernel_spmd

    arrays, shape = host_layout(inputs)
    B, L, D = shape
    E = arrays["router_bias"].shape[0]
    nc = bacc.Bacc("TRN2", target_bir_lowering=False, num_devices=1)
    d, given = {"seq": L}, {}
    for name, a in arrays.items():
        given["in_" + name] = a
        d[name] = nc.dram_tensor("in_" + name, a.shape, mybir.dt.from_np(a.dtype), kind="ExternalInput").ap()
    d["out"] = nc.dram_tensor("out_0", (B * L, D), F32, kind="ExternalOutput").ap()
    build(nc, d, B * L, D, E)
    r = run_bass_kernel_spmd(nc, [given], core_ids=[0])
    return r.results[0]["out_0"].reshape(B, L, D)
```

```python
from contextlib import ExitStack

import numpy as np

import concourse.bass as bass
from concourse import mybir

P = 128
CH = 512
Q = CH // P
EPS = 1e-5
F32, BF16, I32, U32 = mybir.dt.float32, mybir.dt.bfloat16, mybir.dt.int32, mybir.dt.uint32
ALU, ACT, AX = mybir.AluOpType, mybir.ActivationFunctionType, mybir.AxisListType
DP = 96

PE_AT = dict(last=0.5, u=(0, 1, 2, 2.5), y=(1.5, 3, 4.5, 6), conv=(4.0, 4, 5, 5.5), x=6.0, out=(7, 9.5),
             dt=(7.5, 8, 8.0, 9), z=(10.0, 11, 11, 11.5), xn=(11.5, 12.0), skip=(13, 14, 14.5, 15), route=14.0,
             logits=15, c=15.5)
ACT_AT = dict(y=0, u=(2.0, 2.0, 2.5, 3.0), uc=(4.5, 4.5, 6, 6), x=7, dt=(7.5, 8, 8.5, 9), exp=9.5, ln=11.0,
              z=(11.0, 11.0, 12.0, 12.0), xn=(12.5, 13), skip=(13, 14.0, 14.5, 15), probs=15.0, logits=14.5, c=15.5)
DVE_AT = dict(put=1.0, gate=(2.5, 3.5, 5.5, 6.5), halo=7.5, bc=7.5, add=(8, 10.5), norm=10.5, rows=12, e=11.0,
              dtu=13.5, logits=15.0, probs=15.5)
POOL_AT = dict(root=12.5, dt=(13.5, 14.5, 14.5))


class Count:

    def __init__(self, reg, per, base):
        self.reg, self.per, self.base = reg, per, base

    def __mul__(self, k):
        return Count(self.reg, self.per * k, self.base * k)

    def __add__(self, k):
        return Count(self.reg, self.per, self.base + k)

    def value(self):
        return self.base if self.per == 0 else self.reg * self.per + self.base


def wait(eng, sem, count):
    if isinstance(count, int):
        count = Count(None, 0, count)
    assert count.per == 0 or count.base >= 1
    if count.per or count.base > 0:
        eng.wait_ge(sem, count.value())


class Signal:

    def __init__(self, sem, parts=1, ahead=0):
        self.sem, self.parts, self.ahead = sem, parts, ahead

    def count(self, inst, part=None):
        part = self.parts - 1 if part is None else part
        return inst * self.parts + (self.ahead * self.parts + part + 1)

    def wait(self, eng, inst, part=None):
        wait(eng, self.sem, self.count(inst, part))


def placed(at, table, name):
    places = table[name]
    if not isinstance(places, (list, tuple)):
        places = (places,)
    return [j for j, place in enumerate(places) if place == at]


def mamba_phase(nc, d):
    NCH = d["x"].shape[0] // CH - 1
    N = d["A_log"].shape[1]
    D = d["x"].shape[1]
    KD = D // P
    DI = d["W_out"].shape[0]
    M = DI // P
    R = d["W_dt"].shape[0]
    E = d["router_bias"].shape[0]
    TAPS = d["conv_w"].shape[1]
    L = Q - 1
    VM = M // 2
    V = VM * P
    assert M == 4 and KD == 2 and R == 32 and N == 16 and TAPS == 4 and E * Q <= P
    assert NCH % 2 == 0 and d["seq"] == 4 * CH
    assert PE_AT["last"] <= 1

    uses = sorted((at, k, j, name) for k, name in enumerate(("y", "skip", "u", "conv", "out", "z", "x", "c", "dt", "xn",
                                                             "route", "logits"))
                  for j, at in enumerate(PE_AT[name] if isinstance(PE_AT[name], (list, tuple)) else [PE_AT[name]]))
    order = [(name, j) for _, _, j, name in uses]
    bank_of = {use: i % 2 for i, use in enumerate(order)}

    with ExitStack() as ctx:
        def sb(name, shape, dt=F32):
            return ctx.enter_context(nc.sbuf_tensor("sb_" + name, shape, dt))

        def sem(name):
            return ctx.enter_context(nc.semaphore(name))

        def signal(name, parts=1, ahead=0):
            return Signal(sem(name), parts, ahead)

        w_in = sb("w_in", [P, KD, 2 * DI])
        w_x = sb("w_x", [P, M, DP + R])
        w_dt = sb("w_dt", [P, DI])
        w_out = sb("w_out", [P, M, D])
        w_r = sb("w_r", [P, KD, E])
        conv_w = sb("conv_w", [P, M, TAPS])
        conv_d = sb("conv_d", [P, M, TAPS, P])
        conv_b = sb("conv_b", [P, M])
        b_dt = sb("b_dt", [P, M])
        a_neg = sb("a_neg", [P, M, N])
        d_par = sb("d_par", [P, M])
        d_diag = sb("d_diag", [P, M, P])
        ident = sb("ident", [P, P])
        pick = sb("pick", [DP, N, P], BF16)
        nw_row = sb("nw_row", [P, D])
        rb_row = sb("rb_row", [P, E])
        neg_half = sb("neg_half", [P, 2 * Q])
        zeros = sb("zeros", [P, D + 1])
        keep = sb("keep", [P, N * M], I32)
        xT = sb("xT", [P, KD, CH])
        u = sb("u", [P, M, CH + TAPS - 1])
        halo = sb("halo", [P, M, TAPS - 1])
        work = sb("work", [P, M, CH])
        uc = sb("uc", [P, M, CH])
        sz = sb("sz", [P, 2, M, CH])
        dt = sb("dt", [P, 2, M, CH])
        dtu = sb("dtu", [P, 2, M, CH])
        bc = sb("bc", [DP, 2, CH], BF16)
        rest = sb("rest", [P, CH])
        bc_mid = sb("bc_mid", [DP, CH], BF16)
        cT = sb("cT", [P, 2, Q, N])
        b_row = sb("b_row", [P, 4, CH])
        da = sb("da", [P, 2, M, CH])
        h = sb("h", [P, 4, M, CH])
        state = sb("state", [P, N, M])
        yT = sb("yT", [P, 2, Q, DI])
        chT = sb("chT", [P, 2, DI])
        xk = sb("xk", [P, Q, D])
        row = sb("row", [P, Q, D + E])
        xnT = sb("xnT", [P, KD, CH])
        stats = sb("stats", [P, Q, 6])
        mv = sb("mv", [P, Q, 2])
        var_e = sb("var_e", [P, 2, Q])
        rvar = sb("rvar", [P, Q])
        rms = sb("rms", [P, Q])
        scales = sb("scales", [P, 2, Q])
        lg_wide = sb("lg_wide", [P, P])
        lg = lg_wide[:, 0:Q * E].rearrange("p (q e) -> p q e", q=Q)
        lg_max = sb("lg_max", [P, Q])
        lg_d = sb("lg_d", [P, Q, E])
        lg_e = sb("lg_e", [P, Q, E])
        lg_s = sb("lg_s", [P, Q])
        lg_r = sb("lg_r", [P, Q])
        lgT = sb("lgT", [Q * E, P])

        hT_ps = ctx.enter_context(nc.psum_tensor("hT_ps", [P, Q, DI], F32))
        sum_ps = ctx.enter_context(nc.psum_tensor("sum_ps", [P, DI], F32))
        b_ps = ctx.enter_context(nc.psum_tensor("b_ps", [P, CH], F32))
        f_ps = ctx.enter_context(nc.psum_tensor("f_ps", [P, 2, CH], F32))

        def front(name, j=0):
            return f_ps[:, bank_of[name, j], :]

        weights_in, set_up, a_ready = sem("weights_in"), sem("set_up"), sem("a_ready")
        xT_in, xk_in, zeroed, waited = signal("xT_in", 16), signal("xk_in", 16), sem("zeroed"), sem("waited")
        stored, store_free = signal("stored", 48), signal("store_free", 1, 1)
        u_made, u_copied = signal("u_made", M), signal("u_copied", M)
        halo_put, halo_saved = signal("halo_put"), signal("halo_saved")
        conv_made, uc_made = signal("conv_made", M), signal("uc_made", M)
        z_made, z_done = signal("z_made", M), signal("z_done", M)
        xp_made, xp_copied, bc_split = signal("xp_made"), signal("xp_copied", 2), signal("bc_split", 4)
        c_made, c_copied = signal("c_made"), signal("c_copied")
        d_made, d_read, soft = signal("d_made", M), signal("d_read", M), signal("soft", 2)
        w1_made, dt_ops, dtu_made = signal("w1_made"), signal("dt_ops", 3), signal("dtu_made")
        b_made, b_copied = signal("b_made"), signal("b_copied", 1, 1)
        driven, decayed = signal("driven", 1, 4), signal("decayed")
        scanned, carried = signal("scanned", 1, 2), signal("carried", 1, N)
        turned = signal("turned", Q, 4)
        added = signal("added", Q, 1)
        scaled, summed = signal("scaled", 1, 1), signal("summed", 1, 2)
        skipped, skip_copied = signal("skipped", Q + 1), signal("skip_copied", Q, 1)
        sum_copied = signal("sum_copied", 1, 1)
        y_turned, gated = signal("y_turned", M, 1), signal("gated", M, 1)
        o_made, o_read = signal("o_made", 2), signal("o_read", 2, 1)
        ln_ops, pow_made, x1_made, xn_made = (
            signal("ln_ops", 12), signal("pow_made"), signal("x1_made"), signal("xn_made"))
        t_made, t_copied = signal("t_made", KD), signal("t_copied", KD, 1)
        l_made, l_read = signal("l_made"), signal("l_read", 1, 1)
        lt_made, lt_copied = signal("lt_made"), signal("lt_copied", 1, 1)
        sm_ops, ex_made, probs_made = signal("sm_ops", 4), signal("ex_made"), signal("probs_made")
        toggled = signal("toggled")
        with_credit = (store_free, b_copied, driven, scanned, carried, turned, added, scaled, summed, skip_copied,
                       sum_copied, y_turned, gated, o_read, t_copied, l_read, lt_copied)

        def chunk_rows(t, c):
            return t.rearrange("(c q p) d -> c p q d", q=Q, p=P)[c.value()]

        def chunks(eng, body):
            with eng.Fori(0, NCH // 2) as i:
                for par in range(2):
                    body(Count(i, 2, par), par)

        def width(q):
            return V if q == L else DI

        def step(c, n):
            return c * N + n

        def not_first(f):
            return f.per or f.base

        first, final = Count(None, 0, 0), Count(None, 0, NCH)
        weights = (
            (w_in[:], d["W_in"].rearrange("(k p) n -> p k n", p=P)),
            (ident[:], d["ident"]),
            (conv_w[:], d["conv_w"].rearrange("(m p) k -> p m k", p=P)),
            (conv_b[:], d["conv_b"]), (b_dt[:], d["b_dt"]), (d_par[:], d["D_param"]),
            (a_neg[:], d["A_log"].rearrange("(m p) n -> p m n", p=P)),
            (w_x[:], d["W_x"].rearrange("(k p) n -> p k n", p=P)),
            (w_dt[DP:DP + R, :], d["W_dt"]),
            (pick[:], d["pick"][:, 0:N, :]),
            (w_out[:], d["W_out"].rearrange("(k p) n -> p k n", p=P)),
            (w_r[:], d["W_r"].rearrange("(k p) n -> p k n", p=P)),
            (nw_row[:], d["nw_rows"]),
            (rb_row[:], d["rb_rows"]),
        )
        all_weights = 16 * len(weights)
        block = ctx.enter_context(nc.Block())

        @block.sync
        def _(sp):
            def load_xT(f):
                sp.dma_start(xT[:], d["xT"][f.value()]).then_inc(xT_in.sem, 16)

            def load_xk(c):
                sp.dma_start(xk[:], chunk_rows(d["x"], c)).then_inc(xk_in.sem, 16)

            def zero_acc(c):
                sp.dma_start(chunk_rows(d["acc"], c),
                             zeros[:].unsqueeze(1).to_broadcast([P, Q, D + 1])).then_inc(zeroed, 16)

            def store(c):
                x1_made.wait(sp, c)
                sp.dma_start(chunk_rows(d["x1"], c), xk[:]).then_inc(stored.sem, 16)
                lt_copied.wait(sp, c)
                sp.dma_start(d["logits"].rearrange("e (c q p) -> c q e p", q=Q, p=P)[c.value()],
                             lgT[:]).then_inc(stored.sem, 16)
                probs_made.wait(sp, c)
                sp.dma_start(chunk_rows(d["table"], c), row[:]).then_inc(stored.sem, 16)

            load_xT(first)
            for dst, src in weights:
                sp.dma_start(dst, src).then_inc(weights_in, 16)
            load_xk(first)
            z_made.wait(sp, first)
            load_xT(first + 1)
            sp.wait_ge(set_up, 1)

            def body(c, par):
                z_made.wait(sp, c + 1)
                load_xT(c + 2)
                zero_acc(c)
                store(c)
                stored.wait(sp, c)
                sp.sem_inc(store_free.sem, 1)
                load_xk(c + 1)

            chunks(sp, body)
            zero_acc(final)
            store(final)
            stored.wait(sp, final)
            sp.wait_ge(zeroed, 16 * (NCH + 1))

        @block.tensor
        def _(pe):
            def release(use, inst):
                name, j = use
                return {
                    "y": lambda: [(gated, inst, j)], "u": lambda: [(u_copied, inst, j)],
                    "conv": lambda: [(uc_made, inst, j)], "z": lambda: [(z_done, inst, j)],
                    "x": lambda: [(bc_split, inst, 0), (xp_copied, inst, 1)], "c": lambda: [(c_copied, inst, 0)],
                    "dt": lambda: [(d_read, inst, j)], "skip": lambda: [(skip_copied, inst, j)],
                    "out": lambda: [(o_read, inst, j)], "xn": lambda: [(t_copied, inst, j)],
                    "route": lambda: [(l_read, inst, 0)], "logits": lambda: [(lt_copied, inst, 0)],
                }[name]()

            FRONT = ("u", "conv", "z", "x", "c", "dt", "skip")
            pending = {}

            def bank(name, inst, j=0, after=()):
                b = bank_of[name, j]
                latest = {}
                for sig, i, part in [*pending.get(b, ()), *after]:
                    count = sig.count(i, part)
                    if sig.sem.name not in latest or latest[sig.sem.name][1].base < count.base:
                        latest[sig.sem.name] = (sig, count)
                for sig, count in latest.values():
                    wait(pe, sig.sem, count)
                pending[b] = release((name, j), inst)
                return front(name, j)

            def project_u(f, m):
                out = bank("u", f, m, [(xT_in, f, None)])
                for k in range(KD):
                    mm = pe.matmul(out, w_in[:, k, m * P:(m + 1) * P], xT[:, k, :], start=k == 0, stop=k == KD - 1)
                mm.then_inc(u_made.sem, 1)

            def convolve(f, m):
                out = bank("conv", f, m, [(halo_put, f, None), (u_copied, f, m)])
                for k in range(TAPS):
                    mm = pe.matmul(out, conv_d[:, m, k, :], u[:, m, k:k + CH], start=k == 0, stop=k == TAPS - 1)
                mm.then_inc(conv_made.sem, 1)

            def project_z(f, m):
                out = bank("z", f, m, [(xT_in, f, None)])
                for k in range(KD):
                    mm = pe.matmul(out, w_in[:, k, DI + m * P:DI + (m + 1) * P], xT[:, k, :],
                                   start=k == 0, stop=k == KD - 1)
                mm.then_inc(z_made.sem, 1)

            def project_x(f):
                out = bank("x", f, 0, [(uc_made, f, None)])
                for m in range(M):
                    mm = pe.matmul(out, w_x[:, m, :], uc[:, m, :], start=m == 0, stop=m == M - 1)
                mm.then_inc(xp_made.sem, 1)

            def project_c(f):
                out = bank("c", f, 0, [(uc_made, f, None)])
                for q in range(Q):
                    for m in range(M):
                        mm = pe.matmul(out[:, q * N:(q + 1) * N], uc[:, m, q * P:(q + 1) * P], w_x[:, m, N:2 * N],
                                       start=m == 0, stop=m == M - 1)
                mm.then_inc(c_made.sem, 1)

            def project_dt(f, m):
                out = bank("dt", f, m, [(xp_copied, f, None)])
                pe.matmul(out, w_dt[DP:DP + R, m * P:(m + 1) * P], rest[DP:DP + R, :],
                          start=True, stop=True).then_inc(d_made.sem, 1)

            def spread(c, n, par):
                bc_split.wait(pe, c)
                b_copied.wait(pe, step(c, n) + -1)
                pe.matmul(b_ps[:], pick[:, n, :], bc[:, par, :], start=True, stop=True).then_inc(b_made.sem, 1)

            def skip(c, q):
                if q < Q:
                    out = bank("skip", c, q, [(uc_made, c, None)])
                    tiles = range(VM if q == L else M)
                else:
                    uc_made.wait(pe, c)
                    sum_copied.wait(pe, c)
                    out = sum_ps[:]
                    tiles = range(VM, M)
                for m in tiles:
                    mm = pe.matmul(out[:, m * P:(m + 1) * P], uc[:, m, min(q, L) * P:(min(q, L) + 1) * P], d_diag[:, m, :],
                                   start=m == tiles[0], stop=q < Q and m == tiles[-1], skip_group_check=True)
                mm.then_inc(skipped.sem, 1)

            def turn_h(c, n):
                scanned.wait(pe, step(c, n))
                for q in range(Q):
                    added.wait(pe, step(c, n) + -1, q)
                    if q == L:
                        scaled.wait(pe, step(c, n) + -1)
                    for m in range(M):
                        t = pe.transpose(hT_ps[:, q, m * P:(m + 1) * P], h[:, n % 4, m, q * P:(q + 1) * P], ident[:])
                    t.then_inc(turned.sem, 1)

            def sum_last(c, n):
                scaled.wait(pe, step(c, n))
                pe.matmul(sum_ps[:, V:], ident[:], chT[:, n % 2, V:], start=False, stop=n == N - 1,
                          skip_group_check=True).then_inc(summed.sem, 1)

            def turn_y(c, par, m):
                out = bank("y", c, m, [(added, step(c, -1), None), (sum_copied, c, None)])
                for q in range(Q):
                    t = pe.transpose(out[:, q * P:(q + 1) * P], yT[:, 1 - par, q, m * P:(m + 1) * P], ident[:])
                t.then_inc(y_turned.sem, 1)

            def output(c, par, j):
                out = bank("out", c, j, [(gated, c, None)])
                for q in (2 * j, 2 * j + 1):
                    for m in range(M):
                        mm = pe.matmul(out[:, (q % 2) * D:(q % 2 + 1) * D], sz[:, 1 - par, m, q * P:(q + 1) * P],
                                       w_out[:, m, :], start=m == 0, stop=m == M - 1)
                mm.then_inc(o_made.sem, 1)

            def turn_xn(c, k):
                out = bank("xn", c, k, [(xn_made, c, None)])
                for q in range(Q):
                    t = pe.transpose(out[:, q * P:(q + 1) * P], row[:, q, k * P:(k + 1) * P], ident[:])
                t.then_inc(t_made.sem, 1)

            def route(c):
                out = bank("route", c, 0, [(t_copied, c, None)])
                for q in range(Q):
                    for k in range(KD):
                        mm = pe.matmul(out[:, q * E:(q + 1) * E], xnT[:, k, q * P:(q + 1) * P], w_r[:, k, :],
                                       start=k == 0, stop=k == KD - 1)
                mm.then_inc(l_made.sem, 1)

            def turn_logits(c):
                out = bank("logits", c, 0, [(l_read, c, None)])
                pe.transpose(out[:, 0:P], lg_wide[:], ident[:]).then_inc(lt_made.sem, 1)

            pe.wait_ge(weights_in, all_weights)
            pe.wait_ge(set_up, 3)
            for m in range(M):
                project_u(first, m)
            for m in range(M):
                convolve(first, m)
            for m in range(M):
                project_z(first, m)
            project_x(first)
            project_c(first)
            for m in range(M):
                project_dt(first, m)
            for q in range(Q):
                skip(first, q)
            for n in range(4):
                spread(first, n, 0)

            def body(c, par):
                f = c + 1
                for b in range(2):
                    name, j = [use for use in order if bank_of[use] == b][-1]
                    last_use = release((name, j), c if name in FRONT else c + -1)
                    pending[b] = last_use + [(skip_copied, c, L)]

                def others(at):
                    for m in placed(at, PE_AT, "y"):
                        turn_y(c, par, m)
                    for q in placed(at, PE_AT, "skip"):
                        skip(f, q)
                    if placed(at, PE_AT, "last"):
                        skip(c, Q)
                    for m in placed(at, PE_AT, "u"):
                        project_u(f, m)
                    for m in placed(at, PE_AT, "conv"):
                        convolve(f, m)
                    for j in placed(at, PE_AT, "out"):
                        output(c, par, j)
                    for m in placed(at, PE_AT, "z"):
                        project_z(f, m)
                    if placed(at, PE_AT, "x"):
                        project_x(f)
                    if placed(at, PE_AT, "c"):
                        project_c(f)
                    for m in placed(at, PE_AT, "dt"):
                        project_dt(f, m)
                    for k in placed(at, PE_AT, "xn"):
                        turn_xn(c, k)
                    if placed(at, PE_AT, "route"):
                        route(c)
                    if placed(at, PE_AT, "logits"):
                        turn_logits(c)

                for n in range(N):
                    others(n)
                    if n:
                        sum_last(c, n - 1)
                    turn_h(c, n)
                    s = n + 4
                    spread(c if s < N else f, s % N, par if s < N else 1 - par)
                    others(n + 0.5)
                sum_last(c, N - 1)

            chunks(pe, body)
            pending.clear()
            for m in range(M):
                turn_y(final, 0, m)
            for j in range(2):
                output(final, 0, j)
            for k in range(KD):
                turn_xn(final, k)
            route(final)
            turn_logits(final)

        @block.scalar
        def _(act):
            def copy_u(f, m):
                if not_first(f):
                    dt_ops.wait(act, f + -1)
                u_made.wait(act, f, m)
                act.activation(u[:, m, TAPS - 1:], front("u", m), ACT.Copy).then_inc(u_copied.sem, 1)

            def silu_uc(f, m):
                if not_first(f):
                    skipped.wait(act, f + -1)
                    dtu_made.wait(act, f + -1)
                conv_made.wait(act, f, m)
                act.activation(uc[:, m, :], front("conv", m), ACT.Silu, bias=conv_b[:, m:m + 1]).then_inc(uc_made.sem, 1)

            def silu_z(f, par, m):
                if not_first(f):
                    o_made.wait(act, f + -1)
                z_made.wait(act, f, m)
                act.activation(sz[:, par, m, :], front("z", m), ACT.Silu).then_inc(z_done.sem, 1)

            def copy_xp(f, par):
                xp_made.wait(act, f)
                act.activation(rest[DP:DP + R, :], front("x")[DP:DP + R], ACT.Copy).then_inc(xp_copied.sem, 1)
                act.activation(bc[:, par, :], front("x")[0:DP], ACT.Copy).then_inc(xp_copied.sem, 1)

            def copy_c(f, par):
                c_made.wait(act, f)
                act.activation(cT[:, par], front("c")[:, 0:Q * N], ACT.Copy).then_inc(c_copied.sem, 1)

            def parts_dt(f, par, m):
                d_made.wait(act, f, m)
                act.activation(work[:, m, :], front("dt", m), ACT.Abs, bias=b_dt[:, m:m + 1])
                act.activation(dt[:, par, m, :], front("dt", m), ACT.Relu, bias=b_dt[:, m:m + 1]).then_inc(d_read.sem, 1)

            def exp_dt(f):
                d_read.wait(act, f)
                act.activation(work[:], work[:], ACT.Exp, scale=-1.0).then_inc(soft.sem, 1)

            def log_dt(f, par):
                soft.wait(act, f, 0)
                act.activation(dtu[:, par], work[:], ACT.Ln, bias=1.0).then_inc(soft.sem, 1)

            def copy_b(c, n):
                b_made.wait(act, step(c, n))
                driven.wait(act, step(c, n) + -4)
                act.activation(b_row[:, n % 4, :], b_ps[:], ACT.Copy).then_inc(b_copied.sem, 1)

            def decay(c, n, par):
                dt_ops.wait(act, c)
                scanned.wait(act, step(c, n) + -2)
                for m in range(M):
                    e = act.activation(da[:, n % 2, m, :], dt[:, par, m, :], ACT.Exp, scale=a_neg[:, m, n:n + 1])
                e.then_inc(decayed.sem, 1)

            def scale_last(c, n, par):
                if n == 0:
                    c_copied.wait(act, c)
                turned.wait(act, step(c, n), L)
                summed.wait(act, step(c, n) + -2)
                act.activation(chT[:, n % 2, V:], hT_ps[:, L, V:], ACT.Copy,
                               scale=cT[:, par, L, n:n + 1]).then_inc(scaled.sem, 1)

            def copy_skip(c, par, q):
                y_turned.wait(act, c + -1)
                skipped.wait(act, c, q)
                act.activation(yT[:, par, q, 0:width(q)], front("skip", q)[:, 0:width(q)], ACT.Copy).then_inc(skip_copied.sem, 1)

            def copy_sum(c, par):
                summed.wait(act, step(c, -1))
                act.activation(yT[:, 1 - par, L, V:], sum_ps[:, V:], ACT.Copy).then_inc(sum_copied.sem, 1)

            def copy_xnT(c, k):
                t_made.wait(act, c, k)
                act.activation(xnT[:, k, :], front("xn", k), ACT.Copy).then_inc(t_copied.sem, 1)

            def exp_logits(c):
                sm_ops.wait(act, c, 1)
                act.activation(lg_e[:], lg_d[:], ACT.Exp).then_inc(ex_made.sem, 1)

            def copy_lgT(c):
                lt_made.wait(act, c)
                store_free.wait(act, c + -1)
                act.activation(lgT[:], front("logits")[0:Q * E, 0:P], ACT.Copy).then_inc(lt_copied.sem, 1)

            act.wait_ge(weights_in, all_weights)
            act.activation(a_neg[:], a_neg[:], ACT.Exp).then_inc(a_ready, 1)
            act.wait_ge(a_ready, 1)
            act.activation(a_neg[:], a_neg[:], ACT.Copy, scale=-1.0).then_inc(a_ready, 1)
            act.wait_ge(a_ready, 2)
            for m in range(M):
                copy_u(first, m)
            for m in range(M):
                silu_uc(first, m)
            act.wait_ge(set_up, 3)
            for m in range(M):
                silu_z(first, 0, m)
            copy_xp(first, 0)
            copy_c(first, 0)
            for m in range(M):
                parts_dt(first, 0, m)
            exp_dt(first)
            log_dt(first, 0)
            for q in range(Q):
                copy_skip(first, 0, q)
            for n in range(3):
                copy_b(first, n)
            decay(first, 0, 0)
            decay(first, 1, 0)

            def body(c, par):
                f = c + 1

                def others(at):
                    if placed(at, ACT_AT, "y"):
                        copy_sum(c, par)
                    for q in placed(at, ACT_AT, "skip"):
                        copy_skip(f, 1 - par, q)
                    for m in placed(at, ACT_AT, "u"):
                        copy_u(f, m)
                    for m in placed(at, ACT_AT, "uc"):
                        silu_uc(f, m)
                    for m in placed(at, ACT_AT, "z"):
                        silu_z(f, 1 - par, m)
                    if placed(at, ACT_AT, "x"):
                        copy_xp(f, 1 - par)
                    if placed(at, ACT_AT, "c"):
                        copy_c(f, 1 - par)
                    for m in placed(at, ACT_AT, "dt"):
                        parts_dt(f, 1 - par, m)
                    if placed(at, ACT_AT, "exp"):
                        exp_dt(f)
                    if placed(at, ACT_AT, "ln"):
                        log_dt(f, 1 - par)
                    for k in placed(at, ACT_AT, "xn"):
                        copy_xnT(c, k)
                    if placed(at, ACT_AT, "probs"):
                        exp_logits(c)
                    if placed(at, ACT_AT, "logits"):
                        copy_lgT(c)

                for n in range(N):
                    others(n)
                    s = n + 3
                    copy_b(c if s < N else f, s % N)
                    s = n + 2
                    decay(c if s < N else f, s % N, par if s < N else 1 - par)
                    scale_last(c, n, par)
                    others(n + 0.5)

            chunks(act, body)
            copy_sum(final, 0)
            for k in range(KD):
                copy_xnT(final, k)
            exp_logits(final)
            copy_lgT(final)

        @block.vector
        def _(dve):
            def put_halo(f):
                if not_first(f):
                    dt_ops.wait(dve, f + -1)
                dve.tensor_copy(u[:, :, 0:TAPS - 1], halo[:]).then_inc(halo_put.sem, 1)

            def save_halo(f, cut):
                halo_put.wait(dve, f)
                u_copied.wait(dve, f)
                if cut:
                    dve.tensor_tensor(halo[:].bitcast(I32), u[:, :, CH:].bitcast(I32),
                                      keep[:, 0:M * (TAPS - 1)].rearrange("p (m t) -> p m t", m=M),
                                      ALU.bitwise_and).then_inc(halo_saved.sem, 1)
                else:
                    dve.tensor_copy(halo[:], u[:, :, CH:]).then_inc(halo_saved.sem, 1)

            def split_bc(f, par):
                xp_copied.wait(dve, f)
                dve.tensor_tensor(rest[0:DP, :], front("x")[0:DP], bc[:, par, :], ALU.subtract).then_inc(bc_split.sem, 1)
                bc_split.wait(dve, f, 0)
                dve.tensor_copy(bc[32:64, par, :], rest[32:64, :]).then_inc(bc_split.sem, 1)
                dve.tensor_copy(bc_mid[64:96, :], rest[64:96, :]).then_inc(bc_split.sem, 1)
                bc_split.wait(dve, f, 2)
                dve.tensor_tensor(bc[64:96, par, :], rest[64:96, :], bc_mid[64:96, :],
                                  ALU.subtract).then_inc(bc_split.sem, 1)

            def round_trip(f):
                soft.wait(dve, f, 0)
                halo_saved.wait(dve, f)
                conv_made.wait(dve, f)
                dve.tensor_scalar(u[:, :, 0:CH], work[:], 1.0, -1.0, ALU.add, ALU.add).then_inc(w1_made.sem, 1)

            def dt_times_u(f, par):
                dt_ops.wait(dve, f)
                dve.tensor_tensor(dtu[:, par], dt[:, par], uc[:], ALU.mult).then_inc(dtu_made.sem, 1)

            def scan(c, n):
                decayed.wait(dve, step(c, n))
                driven.wait(dve, step(c, n))
                carried.wait(dve, step(c, n) + -N)
                for m in range(M):
                    op = dve.tensor_tensor_scan(h[:, n % 4, m, :], da[:, n % 2, m, :], h[:, n % 4, m, :],
                                                state[:, n, m:m + 1], ALU.mult, ALU.add)
                op.then_inc(scanned.sem, 1)

            def carry(c, n, cut):
                scanned.wait(dve, step(c, n))
                last = h[:, n % 4, :, CH - 1:CH]
                out = state[:, n, :].unsqueeze(2)
                if cut:
                    op = dve.tensor_tensor(out.bitcast(I32), last.bitcast(I32), keep[:, 0:M].unsqueeze(2),
                                           ALU.bitwise_and)
                else:
                    op = dve.tensor_copy(out, last)
                op.then_inc(carried.sem, 1)

            def add_state(c, n, par):
                if n == 0:
                    c_copied.wait(dve, c)
                for q in range(Q):
                    w = width(q)
                    if n == 0:
                        skip_copied.wait(dve, c, q)
                    turned.wait(dve, step(c, n), q)
                    if q == L:
                        scaled.wait(dve, step(c, n))
                    added.wait(dve, step(c, n) + -1, q)
                    dve.scalar_tensor_tensor(yT[:, par, q, 0:w], hT_ps[:, q, 0:w], cT[:, par, q, n:n + 1], yT[:, par, q, 0:w],
                                             ALU.mult, ALU.add).then_inc(added.sem, 1)

            def gate(c, par, m):
                y_turned.wait(dve, c, m)
                z_done.wait(dve, c)
                dve.tensor_tensor(sz[:, 1 - par, m, :], front("y", m), sz[:, 1 - par, m, :], ALU.mult).then_inc(gated.sem, 1)

            def add_residual(c, j):
                xk_in.wait(dve, c)
                o_made.wait(dve, c, j)
                part = xk[:, 2 * j:2 * j + 2, :].rearrange("p q d -> p (q d)")
                dve.tensor_tensor(part, front("out", j), part, ALU.add).then_inc(o_read.sem, 1)

            def normalize(c):
                for q in range(Q):
                    o_read.wait(dve, c, q // 2)
                    dve.bn_stats(stats[:, q, :], xk[:, q, :]).then_inc(ln_ops.sem, 1)
                ln_ops.wait(dve, c, Q - 1)
                dve.sem_inc(waited, 1)
                for q in range(Q):
                    dve.bn_aggr(mv[:, q, :], stats[:, q, :]).then_inc(ln_ops.sem, 1)
                ln_ops.wait(dve, c, 7)
                dve.tensor_scalar(var_e[:, 0, :], mv[:, :, 1], EPS, None, ALU.add).then_inc(ln_ops.sem, 1)
                ln_ops.wait(dve, c, 8)
                dve.reciprocal(rvar[:], var_e[:, 0, :]).then_inc(ln_ops.sem, 1)
                ln_ops.wait(dve, c, 9)
                dve.tensor_tensor(rms[:], rvar[:], mv[:, :, 1], ALU.mult).then_inc(ln_ops.sem, 1)
                ln_ops.wait(dve, c, 10)
                dve.tensor_scalar(var_e[:, 1, :], rms[:], EPS, None, ALU.add).then_inc(ln_ops.sem, 1)

            def scale_rows(c):
                pow_made.wait(dve, c)
                store_free.wait(dve, c + -1)
                for q in range(Q):
                    op = dve.tensor_scalar(xk[:, q, :], xk[:, q, :], mv[:, q, 0:1], scales[:, 0, q:q + 1],
                                           ALU.subtract, ALU.mult)
                op.then_inc(x1_made.sem, 1)
                x1_made.wait(dve, c)
                for q in range(Q):
                    op = dve.scalar_tensor_tensor(row[:, q, 0:D], xk[:, q, :], scales[:, 1, q:q + 1], nw_row[:],
                                                  ALU.mult, ALU.mult)
                op.then_inc(xn_made.sem, 1)

            def logits(c):
                l_made.wait(dve, c)
                dve.tensor_tensor(lg, front("route")[:, 0:Q * E].rearrange("p (q e) -> p q e", q=Q),
                                  rb_row[:].unsqueeze(1).to_broadcast([P, Q, E]), ALU.add).then_inc(l_read.sem, 1)
                l_read.wait(dve, c)
                dve.tensor_reduce(lg_max[:], lg, AX.X, ALU.max).then_inc(sm_ops.sem, 1)
                sm_ops.wait(dve, c, 0)
                dve.tensor_tensor(lg_d[:], lg, lg_max[:].unsqueeze(2).to_broadcast([P, Q, E]),
                                  ALU.subtract).then_inc(sm_ops.sem, 1)

            def softmax(c):
                ex_made.wait(dve, c)
                dve.tensor_reduce(lg_s[:], lg_e[:], AX.X, ALU.add).then_inc(sm_ops.sem, 1)
                sm_ops.wait(dve, c, 2)
                dve.reciprocal(lg_r[:], lg_s[:]).then_inc(sm_ops.sem, 1)
                sm_ops.wait(dve, c, 3)
                dve.tensor_tensor(row[:, :, D:], lg_e[:], lg_r[:].unsqueeze(2).to_broadcast([P, Q, E]),
                                  ALU.mult).then_inc(probs_made.sem, 1)

            dve.memset(zeros[:], 0.0).then_inc(set_up, 1)
            dve.memset(neg_half[:], -0.5)
            dve.memset(halo[:], 0.0)
            dve.memset(lg_wide[:], 0.0)
            dve.memset(state[:], 0.0)
            dve.memset(keep[:], -1)
            dve.memset(sz[:, 1], 0.0)
            dve.memset(yT[:, 1], 0.0)
            dve.memset(sum_ps[:], 0.0).then_inc(set_up, 1)
            for sig in with_credit:
                dve.sem_inc(sig.sem, sig.parts * sig.ahead)
            dve.wait_ge(weights_in, all_weights)
            for m in range(M):
                for k in range(TAPS):
                    dve.tensor_scalar(conv_d[:, m, k, :], ident[:], conv_w[:, m, k:k + 1], None, ALU.mult)
                op = dve.tensor_scalar(d_diag[:, m, :], ident[:], d_par[:, m:m + 1], None, ALU.mult)
            op.then_inc(set_up, 1)
            dve.wait_ge(set_up, 3)
            put_halo(first)
            save_halo(first, False)
            split_bc(first, 0)
            round_trip(first)
            dt_times_u(first, 0)

            def body(c, par):
                f = c + 1

                def others(at):
                    for m in placed(at, DVE_AT, "gate"):
                        gate(c, par, m)
                    if placed(at, DVE_AT, "put"):
                        put_halo(f)
                    if placed(at, DVE_AT, "halo"):
                        save_halo(f, par == 0)
                    for j in placed(at, DVE_AT, "add"):
                        add_residual(c, j)
                    if placed(at, DVE_AT, "norm"):
                        normalize(c)
                    if placed(at, DVE_AT, "rows"):
                        scale_rows(c)
                    if placed(at, DVE_AT, "bc"):
                        split_bc(f, 1 - par)
                    if placed(at, DVE_AT, "e"):
                        round_trip(f)
                    if placed(at, DVE_AT, "dtu"):
                        dt_times_u(f, 1 - par)
                    if placed(at, DVE_AT, "logits"):
                        logits(c)
                    if placed(at, DVE_AT, "probs"):
                        softmax(c)

                for n in range(N):
                    others(n)
                    scan(c, n)
                    if n:
                        add_state(c, n - 1, par)
                        carry(c, n - 1, par == 1)
                    others(n + 0.5)
                carry(c, N - 1, par == 1)
                add_state(c, N - 1, par)
                if par == 1:
                    carried.wait(dve, step(c, N - 1))
                    halo_saved.wait(dve, f)
                    dve.tensor_scalar(keep[:], keep[:], -1, None, ALU.bitwise_xor).then_inc(toggled.sem, 1)
                    toggled.wait(dve, Count(c.reg, 1, 0))

            chunks(dve, body)
            for m in range(M):
                gate(final, 0, m)
            for j in range(2):
                add_residual(final, j)
            normalize(final)
            scale_rows(final)
            logits(final)
            softmax(final)

        @block.gpsimd
        def _(pool):
            def drive(c, n, par):
                dtu_made.wait(pool, c)
                b_copied.wait(pool, step(c, n))
                turned.wait(pool, step(c, n) + -4)
                carried.wait(pool, step(c, n) + -4)
                pool.tensor_tensor(h[:, n % 4], dtu[:, par], b_row[:, n % 4, :].unsqueeze(1).to_broadcast([P, M, CH]),
                                   ALU.mult).then_inc(driven.sem, 1)

            def sum_dt(f, par, j):
                if j == 0:
                    w1_made.wait(pool, f)
                    soft.wait(pool, f)
                    op = pool.tensor_tensor(work[:], work[:], u[:, :, 0:CH], ALU.subtract)
                if j == 1:
                    op = pool.tensor_tensor(dt[:, par], dt[:, par], dtu[:, par], ALU.add)
                if j == 2:
                    dt_ops.wait(pool, f, 1)
                    op = pool.tensor_tensor(dt[:, par], dt[:, par], work[:], ALU.add)
                op.then_inc(dt_ops.sem, 1)

            def roots(c):
                ln_ops.wait(pool, c)
                pool.tensor_tensor(scales[:].rearrange("p a q -> p (a q)"), var_e[:].rearrange("p a q -> p (a q)"),
                                   neg_half[:], ALU.pow).then_inc(pow_made.sem, 1)

            pool.wait_ge(set_up, 3)
            for j in range(3):
                sum_dt(first, 0, j)

            def body(c, par):
                for n in range(N):
                    drive(c, n, par)
                    if placed(n + 0.5, POOL_AT, "root"):
                        roots(c)
                    for j in placed(n + 0.5, POOL_AT, "dt"):
                        sum_dt(c + 1, 1 - par, j)

            chunks(pool, body)
            roots(final)


def experts_phase(nc, d):
    E = d["logits"].shape[0]
    T = d["logits"].shape[1] - CH
    D = d["x"].shape[1]
    KD = D // P
    F = d["W1"].shape[3]
    FT = F // P
    K = max(1, -(-T // E))
    J = P // E
    TJ = T // J
    NB = TJ // P
    KT = K // P
    HT = min(KT, CH // P)
    HALVES = KT // HT
    HW = HT * P
    NCK = NB * J
    assert K % P == 0 and TJ % P == 0 and NCK + Q <= 256 and KT % HT == 0

    with ExitStack() as ctx:
        def sb(name, shape, dt=F32):
            return ctx.enter_context(nc.sbuf_tensor("sb_" + name, shape, dt))

        def sem(name):
            return ctx.enter_context(nc.semaphore(name))

        slot_lo = sb("slot_lo", [P, NB, P], BF16)
        slot_hi = sb("slot_hi", [P, NB, P], BF16)
        same = sb("same", [P, P])
        before = sb("before", [P, P])
        ident = sb("ident2", [P, P])
        ident_h = sb("ident_h", [P, P], BF16)

        with ExitStack() as ctx2:
            def sb2(name, shape, dt=F32):
                return ctx2.enter_context(nc.sbuf_tensor("sb_" + name, shape, dt))

            def sem2(name):
                return ctx2.enter_context(nc.semaphore(name))

            lg = sb2("lg_all", [P, TJ])
            above = sb2("above", [P, TJ])
            tied = sb2("tied", [P, TJ])
            n_above = sb2("n_above", [P, TJ])
            n_tied = sb2("n_tied", [P, TJ])
            slot_i = sb2("slot_i", [P, TJ], I32)
            part_i = sb2("part_i", [P, 2, TJ], I32)
            part_h = sb2("part_h", [P, 2, TJ], BF16)
            one = sb2("one", [P, 1])
            key, cand = sb2("key", [P, 1], I32), sb2("cand", [P, 1], I32)
            bit = sb2("bit", [P, 2], I32)
            take = sb2("take", [P, 1], I32)
            counts = sb2("counts", [P, 2])
            before_n = sb2("before_n", [P, 2])
            need = sb2("need", [P, 1])
            cnt_ps = ctx2.enter_context(nc.psum_tensor("cnt_ps", [P, CH], F32))
            cut_ps = ctx2.enter_context(nc.psum_tensor("cut_ps", [P, 2, 8 * P], BF16))
            tk_in, tk_set, key_ops, counted, totalled, cut_ops, listed = (
                sem2("tk_in"), sem2("tk_set"), sem2("key_ops"), sem2("counted"), sem2("totalled"),
                sem2("cut_ops"), sem2("listed"))
            cut_made, cut_copied = sem2("cut_made"), sem2("cut_copied")
            OPS = 4
            ROUNDS = 31
            GRP = min(NB, 8)

            with nc.Block() as block:
                @block.sync
                def _(sp):
                    sp.dma_start(lg[:], d["logits"][:, CH:].rearrange("e (j t) -> e j t", j=J)).then_inc(tk_in, 16)
                    for dst, src in ((same, "same"), (before, "before"), (ident, "ident"), (ident_h, "ident_h")):
                        sp.dma_start(dst[:], d[src]).then_inc(tk_in, 16)

                @block.vector
                def _(dve):
                    def count_at_least():
                        dve.tensor_scalar(above[:], lg[:], cand[:].bitcast(F32), 0.0, ALU.is_ge, ALU.add,
                                          accum_out=counts[:, 0:1]).then_inc(counted, 1)

                    dve.memset(cand[:], 0)
                    dve.memset(one[:], 1.0)
                    dve.memset(bit[:, 0:1], 2 ** 30)
                    dve.memset(bit[:, 1:2], 2 ** 29).then_inc(tk_set, 1)
                    dve.wait_ge(tk_set, 1)
                    dve.wait_ge(tk_in, 80)
                    count_at_least()
                    dve.wait_ge(totalled, 1)
                    dve.tensor_scalar(key[:], cnt_ps[:, 0:1], float(K), -1.0, ALU.is_lt, ALU.mult).then_inc(key_ops, 1)
                    dve.wait_ge(key_ops, 1)
                    dve.tensor_tensor(cand[:], key[:], bit[:, 0:1], ALU.bitwise_xor).then_inc(key_ops, 1)
                    with dve.Fori(0, ROUNDS) as r:
                        round_ = Count(r, OPS, 2)
                        wait(dve, key_ops, round_)
                        count_at_least()
                        wait(dve, totalled, Count(r, 1, 2))
                        dve.tensor_scalar(take[:], cnt_ps[:, 0:1], float(K), -1.0, ALU.is_ge,
                                          ALU.mult).then_inc(key_ops, 1)
                        wait(dve, key_ops, round_ + 1)
                        dve.scalar_tensor_tensor(key[:], take[:], bit[:, 0:1], key[:], ALU.bitwise_and,
                                                 ALU.bitwise_xor).then_inc(key_ops, 1)
                        wait(dve, key_ops, round_ + 2)
                        dve.tensor_tensor(cand[:], key[:], bit[:, 1:2], ALU.bitwise_xor).then_inc(key_ops, 1)
                        wait(dve, key_ops, round_ + 3)
                        dve.tensor_scalar(bit[:], bit[:], 1, None, ALU.logical_shift_right).then_inc(key_ops, 1)

                    thr, done = key, 2 + OPS * ROUNDS
                    dve.wait_ge(key_ops, done)
                    dve.tensor_scalar(above[:], lg[:], thr[:].bitcast(F32), 0.0, ALU.is_gt, ALU.add,
                                      accum_out=counts[:, 0:1])
                    dve.tensor_scalar(tied[:], lg[:], thr[:].bitcast(F32), 0.0, ALU.is_equal, ALU.add,
                                      accum_out=counts[:, 1:2]).then_inc(counted, 1)
                    dve.wait_ge(totalled, 33)
                    dve.tensor_copy(before_n[:], cnt_ps[:, 2:4])
                    dve.tensor_scalar(need[:], cnt_ps[:, 0:1], -1.0, float(K), ALU.mult, ALU.add).then_inc(cut_ops, 1)
                    dve.wait_ge(cut_ops, 1)
                    ones = one[:].to_broadcast([P, TJ])
                    dve.tensor_tensor_scan(n_above[:], ones, above[:], before_n[:, 0:1], ALU.mult, ALU.add)
                    dve.tensor_tensor_scan(n_tied[:], ones, tied[:], before_n[:, 1:2], ALU.mult,
                                           ALU.add).then_inc(cut_ops, 1)
                    dve.wait_ge(cut_ops, 2)
                    dve.scalar_tensor_tensor(tied[:], n_tied[:], need[:], tied[:], ALU.is_le, ALU.mult)
                    dve.scalar_tensor_tensor(n_above[:], n_tied[:], need[:], n_above[:], ALU.min,
                                             ALU.add).then_inc(cut_ops, 1)
                    dve.wait_ge(cut_ops, 3)
                    dve.tensor_tensor(above[:], above[:], tied[:], ALU.add).then_inc(cut_ops, 1)
                    dve.wait_ge(cut_ops, 4)
                    dve.tensor_tensor(above[:], above[:], n_above[:], ALU.mult).then_inc(cut_ops, 1)
                    dve.wait_ge(cut_ops, 5)
                    dve.tensor_scalar(slot_i[:], above[:], float(P - 1), None, ALU.add).then_inc(cut_ops, 1)
                    dve.wait_ge(cut_ops, 6)
                    dve.tensor_scalar(part_i[:, 0], slot_i[:], P - 1, None, ALU.bitwise_and)
                    dve.tensor_scalar(part_i[:, 1], slot_i[:], 7, None, ALU.logical_shift_right).then_inc(cut_ops, 1)
                    dve.wait_ge(cut_ops, 7)
                    dve.tensor_copy(part_h[:], part_i[:]).then_inc(cut_ops, 1)
                    n = 0
                    for dst in (slot_lo, slot_hi):
                        for b in range(0, NB, GRP):
                            n += 1
                            dve.wait_ge(cut_made, n)
                            dve.tensor_copy(dst[:, b:b + GRP, :].rearrange("p b e -> p (b e)"),
                                            cut_ps[:, n % 2, 0:GRP * P]).then_inc(cut_copied, 1)

                @block.tensor
                def _(pe):
                    pe.wait_ge(tk_in, 80)
                    with pe.Fori(0, 32) as r:
                        wait(pe, counted, Count(r, 1, 1))
                        pe.matmul(cnt_ps[:, 0:1], same[:], counts[:, 0:1], start=True, stop=True).then_inc(totalled, 1)
                    pe.wait_ge(counted, 33)
                    pe.matmul(cnt_ps[:, 0:2], same[:], counts[:], start=True, stop=True)
                    pe.matmul(cnt_ps[:, 2:4], before[:], counts[:], start=True, stop=True).then_inc(totalled, 1)
                    pe.wait_ge(cut_ops, 8)
                    n = 0
                    for part in range(2):
                        for b in range(0, NB, GRP):
                            n += 1
                            if n > 2:
                                pe.wait_ge(cut_copied, n - 2)
                            for g in range(GRP):
                                t = pe.transpose(cut_ps[:, n % 2, g * P:(g + 1) * P],
                                                 part_h[:, part, (b + g) * P:(b + g + 1) * P], ident_h[:])
                            t.then_inc(cut_made, 1)

        iota_lo = sb("iota_lo", [P, P, J], BF16)
        iota_hi = sb("iota_hi", [P, KT, J], BF16)
        block_no = sb("block_no", [P, NB, J], BF16)
        part_no = sb("part_no", [P, 1])
        b1 = sb("b1", [P, 2, FT])
        b2 = sb("b2", [P, 2, D])
        w1 = sb("w1", [P, 2, KD, F])
        w2 = sb("w2", [P, 2, FT, D])
        hot_lo = sb("hot_lo", [P, P, NB, J], BF16)
        hot_hi = sb("hot_hi", [P, KT, NB, J], BF16)
        where = sb("where", [P, 2, KT, NB, J], BF16)
        where_f = sb("where_f", [P, KT])
        idx = sb("idx", [P, 2, KT], I32)
        rows = sb("rows", [P, 2, KT, D + E])
        gates = sb("gates", [P, 2, KT])
        xeT = sb("xeT", [P, 2, KD, K])
        hT = sb("hT", [P, FT, K])
        yb = sb("yb", [P, KT, D])
        give = sb("give", [P, 2, KT, D + 1])
        list_ps = ctx.enter_context(nc.psum_tensor("list_ps", [P, CH], F32))[:, 0:2 * KT]
        turn_ps = ctx.enter_context(nc.psum_tensor("turn_ps", [P, 2, HW], F32))
        h_ps = ctx.enter_context(nc.psum_tensor("h_ps", [P, 2, CH], F32))
        o_ps = ctx.enter_context(nc.psum_tensor("o_ps", [P, 2, 2, D], F32))
        ex_in, w_in, hots, list_made, idx_ops, gathered, gates_made = (
            sem("ex_in"), (sem("even_w_in"), sem("odd_w_in")), sem("hots"), sem("list_made"), sem("idx_ops"), sem("gathered"),
            sem("gates_made"))
        turned, turn_copied, fc1_made, gelu_made, fc2_made, bias_added, given, added, waited = (
            sem("turned"), sem("turn_copied"), sem("fc1_made"), sem("gelu_made"), sem("fc2_made"),
            sem("bias_added"), sem("given"), sem("added"), sem("waited"))
        PAIRS = -(-KT // 2)
        TURNS = HALVES * KD

        def pair_no(e, par):
            return Count(e.reg, e.per // 2, (e.base - par) // 2 + 1)

        def experts(eng, body):
            for par in range(2):
                body(Count(None, 0, par), par, False)
            with eng.Fori(0, E // 2 - 2) as i:
                for par in range(2):
                    body(Count(i, 2, par + 2), par, False)
            for par in range(2):
                body(Count(None, 0, E - 2 + par), par, par == 1)

        NC2 = 4
        with nc.Block() as block:
            @block.sync
            def _(sp):
                def load(e, par):
                    for dst, src in ((w1, "W1"), (b1, "b1"), (w2, "W2"), (b2, "b2_rows")):
                        sp.dma_start(dst[:, par], d[src][e.value()]).then_inc(w_in[par], 16)

                for dst, src in ((iota_lo, "iota_lo"), (iota_hi, "iota_hi"), (block_no, "block_no"),
                                 (part_no, "part_no")):
                    sp.dma_start(dst[:], d[src]).then_inc(ex_in, 16)
                load(Count(None, 0, 0), 0)
                load(Count(None, 0, 1), 1)

                def body(e, par, last):
                    if e.per or e.base < E - 2:
                        wait(sp, bias_added, (e + 1) * PAIRS)
                        load(e + 2, par)

                experts(sp, body)

            @block.tensor
            def _(pe):
                def make_list(e):
                    wait(pe, hots, (e + 1) * 4)
                    if e.per or e.base:
                        wait(pe, idx_ops, e * 2)
                    for ck in range(NCK):
                        mm = pe.matmul(list_ps, hot_lo[:].rearrange("p i b j -> p i (b j)")[:, :, ck],
                                       where[:].rearrange("p a i b j -> p (a i) (b j)")[:, :, ck],
                                       start=ck == 0, stop=ck == NCK - 1)
                    mm.then_inc(list_made, 1)

                def turn(e, par):
                    wait(pe, gathered, (e + 1) * (16 * KT))
                    for n in range(TURNS):
                        hf, k = divmod(n, KD)
                        if e.per or e.base or n >= 2:
                            wait(pe, turn_copied, e * TURNS + (n - 1))
                        for q in range(HT):
                            t = pe.transpose(turn_ps[:, n % 2, q * P:(q + 1) * P],
                                             rows[:, par, hf * HT + q, k * P:(k + 1) * P], ident[:])
                        t.then_inc(turned, 1)

                def fc1(e, par):
                    wait(pe, w_in[par], pair_no(e, par) * 64)
                    for hf in range(HALVES):
                        wait(pe, turn_copied, e * TURNS + (hf + 1) * KD)
                        for f in range(FT):
                            n = hf * FT + f
                            if e.per or e.base or n >= 2:
                                wait(pe, gelu_made, e * (HALVES * FT) + (n - 1))
                            for k in range(KD):
                                mm = pe.matmul(h_ps[:, n % 2, 0:HW], w1[:, par, k, f * P:(f + 1) * P],
                                               xeT[:, par, k, hf * HW:(hf + 1) * HW], start=k == 0, stop=k == KD - 1)
                            mm.then_inc(fc1_made, 1)

                def fc2(e, par):
                    for q in range(KT):
                        if q % HT == 0:
                            wait(pe, gelu_made, e * (HALVES * FT) + (q // HT + 1) * FT)
                        n = q // 2
                        if q % 2 == 0 and (e.per or e.base or n >= 2):
                            wait(pe, bias_added, e * PAIRS + (n - 1))
                        for f in range(FT):
                            mm = pe.matmul(o_ps[:, n % 2, q % 2, :], hT[:, f, q * P:(q + 1) * P], w2[:, par, f, :],
                                           start=f == 0, stop=f == FT - 1)
                        if q % 2 or q == KT - 1:
                            mm.then_inc(fc2_made, 1)

                first = Count(None, 0, 0)
                make_list(first)
                turn(first, 0)

                def body(e, par, last):
                    fc1(e, par)
                    if not last:
                        make_list(e + 1)
                    fc2(e, par)
                    if not last:
                        turn(e + 1, 1 - par)

                experts(pe, body)

            @block.scalar
            def _(act):
                def copy_turn(e, par):
                    if e.per or e.base > 1:
                        wait(act, fc1_made, (e + -1) * (HALVES * FT))
                    for n in range(TURNS):
                        hf, k = divmod(n, KD)
                        wait(act, turned, e * TURNS + (n + 1))
                        act.activation(xeT[:, par, k, hf * HW:(hf + 1) * HW], turn_ps[:, n % 2, :],
                                       ACT.Copy).then_inc(turn_copied, 1)

                def gelu(e, par):
                    if e.per or e.base:
                        wait(act, fc2_made, e * PAIRS)
                    for hf in range(HALVES):
                        for f in range(FT):
                            n = hf * FT + f
                            wait(act, fc1_made, e * (HALVES * FT) + (n + 1))
                            act.activation(hT[:, f, hf * HW:(hf + 1) * HW], h_ps[:, n % 2, 0:HW], ACT.Gelu,
                                           bias=b1[:, par, f:f + 1]).then_inc(gelu_made, 1)

                def times_gate(e, par):
                    wait(act, gates_made, (e + 1) * 1)
                    if e.per or e.base > 1:
                        wait(act, added, (e + -1) * (16 * KT))
                    for n in range(PAIRS):
                        wait(act, bias_added, e * PAIRS + (n + 1))
                        for q in range(2 * n, min(2 * n + 2, KT)):
                            op = act.activation(give[:, par, q, 0:D], yb[:, q, :], ACT.Copy,
                                                scale=gates[:, par, q:q + 1])
                        op.then_inc(given, 1)

                first = Count(None, 0, 0)
                act.wait_ge(ex_in, 16 * NC2)
                copy_turn(first, 0)

                def body(e, par, last):
                    gelu(e, par)
                    times_gate(e, par)
                    if not last:
                        copy_turn(e + 1, 1 - par)

                experts(act, body)

            @block.vector
            def _(dve):
                def make_hots(e):
                    if e.per or e.base:
                        wait(dve, list_made, e * 1)
                    lo = slot_lo[:].rearrange("p b (e j) -> p e b j", e=E)[:, e.value()]
                    hi = slot_hi[:].rearrange("p b (e j) -> p e b j", e=E)[:, e.value()]
                    dve.tensor_tensor(hot_hi[:], hi.unsqueeze(1).to_broadcast([P, KT, NB, J]),
                                      iota_hi[:].unsqueeze(2).to_broadcast([P, KT, NB, J]),
                                      ALU.is_equal).then_inc(hots, 1)
                    dve.tensor_tensor(hot_lo[:], lo.unsqueeze(1).to_broadcast([P, P, NB, J]),
                                      iota_lo[:].unsqueeze(2).to_broadcast([P, P, NB, J]),
                                      ALU.is_equal).then_inc(hots, 1)
                    wait(dve, hots, e * 4 + 1)
                    dve.tensor_scalar(where[:, 0], hot_hi[:], part_no[:], None, ALU.mult).then_inc(hots, 1)
                    dve.tensor_tensor(where[:, 1], hot_hi[:], block_no[:].unsqueeze(1).to_broadcast([P, KT, NB, J]),
                                      ALU.mult).then_inc(hots, 1)

                def make_idx(e, par):
                    wait(dve, list_made, e * 1 + 1)
                    if e.per or e.base > 1:
                        wait(dve, added, (e + -1) * (16 * KT))
                    dve.tensor_copy(where_f[:], list_ps[:, 0:KT]).then_inc(idx_ops, 1)
                    wait(dve, idx_ops, e * 2 + 1)
                    dve.scalar_tensor_tensor(idx[:, par, :], list_ps[:, KT:], float(P), where_f[:], ALU.mult,
                                             ALU.add).then_inc(idx_ops, 1)

                def copy_gates(e, par):
                    wait(dve, gathered, (e + 1) * (16 * KT))
                    if e.per or e.base > 1:
                        wait(dve, added, (e + -1) * (16 * KT))
                        wait(dve, given, (e + -1) * PAIRS)
                    col = rows[:, par].rearrange("p k d -> p d k")[:, D:, :][:, e.value(), :]
                    dve.tensor_copy(gates[:, par, :], col)
                    dve.tensor_copy(give[:, par, :, D], col).then_inc(gates_made, 1)

                def add_bias(e, par):
                    if e.per or e.base:
                        wait(dve, given, e * PAIRS)
                    for n in range(PAIRS):
                        w = min(2, KT - 2 * n)
                        wait(dve, fc2_made, e * PAIRS + (n + 1))
                        dve.tensor_tensor(yb[:, 2 * n:2 * n + w, :], o_ps[:, n % 2, 0:w, :],
                                          b2[:, par, :].unsqueeze(1).to_broadcast([P, w, D]),
                                          ALU.add).then_inc(bias_added, 1)

                dve.wait_ge(ex_in, 16 * NC2)
                first = Count(None, 0, 0)
                make_hots(first)
                make_idx(first, 0)

                def body(e, par, last):
                    copy_gates(e, par)
                    if not last:
                        make_hots(e + 1)
                        make_idx(e + 1, 1 - par)
                    add_bias(e, par)

                experts(dve, body)

            @block.gpsimd
            def _(pool):
                def gather(e, par):
                    wait(pool, idx_ops, (e + 1) * 2)
                    if e.per or e.base > 1:
                        wait(pool, turned, (e + -1) * TURNS)
                        wait(pool, gates_made, (e + -1) * 1)
                    pool.sem_inc(waited, 1)
                    for q in range(KT):
                        pool.indirect_dma_start(
                            out=rows[:, par, q, :], out_offset=None, in_=d["table"],
                            in_offset=bass.IndirectOffsetOnAxis(ap=idx[:, par, q:q + 1], axis=0)).then_inc(gathered, 16)

                def scatter(e, par):
                    if e.per or e.base:
                        wait(pool, added, e * (16 * KT))
                    wait(pool, given, (e + 1) * PAIRS)
                    pool.sem_inc(waited, 1)
                    for q in range(KT):
                        pool.indirect_dma_start(
                            out=d["acc"], out_offset=bass.IndirectOffsetOnAxis(ap=idx[:, par, q:q + 1], axis=0),
                            in_=give[:, par, q, :], in_offset=None,
                            compute_op=ALU.add).then_inc(added, 16)

                gather(Count(None, 0, 0), 0)

                def body(e, par, last):
                    if not last:
                        gather(e + 1, 1 - par)
                    scatter(e, par)

                experts(pool, body)
                pool.wait_ge(added, E * 16 * KT)


def final_phase(nc, d):
    T, D = d["out"].shape
    R = 4
    NI = T // CH // R

    with ExitStack() as ctx:
        def sb(name, shape, dt=F32):
            return ctx.enter_context(nc.sbuf_tensor("sb_" + name, shape, dt))

        def sem(name):
            return ctx.enter_context(nc.semaphore(name))

        acc = sb("acc_f", [P, R, Q, D + 1])
        x1 = sb("x1_f", [P, R, Q, D])
        out = sb("out_f", [P, R, Q, D])
        none = sb("none_f", [P, R, Q])
        gate_r = sb("gate_r", [P, R, Q])
        stats = sb("stats_f", [P, R, Q, 6])
        mv = sb("mv_f", [P, R, Q, 2])
        var_e = sb("var_e_f", [P, R, Q])
        rstd = sb("rstd_f", [P, R, Q])
        shift = sb("shift_f", [P, R, Q])
        neg_half = sb("neg_half_f", [P, Q])
        loaded = [sem(f"loaded_{r}") for r in range(R)]
        left = [sem(f"left_{r}") for r in range(R)]
        half_set, combine_ops, combined, stats_ops, stats_seen, rooted, shifts, shifted, normed = (
            sem("half_set"), sem("combine_ops"), sem("combined"), sem("stats_ops"), sem("stats_seen_f"), sem("rooted"),
            sem("shifts"), sem("shifted"), sem("normed"))

        def rounds(eng, body):
            body(None)
            with eng.Fori(0, NI - 1) as i:
                body(i)

        def number(i, r):
            return Count(None, 0, r) if i is None else Count(i, R, R + r)

        def turn(i):
            return Count(None, 0, 0) if i is None else Count(i, 1, 1)

        def rows_of(t, c):
            return t.rearrange("(c q p) d -> c p q d", q=Q, p=P)[c.value()]

        with nc.Block() as block:
            @block.sync
            def _(sp):
                def load(c, r):
                    sp.dma_start(acc[:, r], rows_of(d["acc"], c + 1)).then_inc(loaded[r], 16)
                    sp.dma_start(x1[:, r], rows_of(d["x1"], c + 1)).then_inc(loaded[r], 16)

                for r in range(R):
                    load(Count(None, 0, r), r)

                with sp.Fori(0, NI - 1) as i:
                    for r in range(R):
                        wait(sp, normed, Count(i, R, r + 1))
                        load(Count(i, R, R + r), r)

            @block.vector
            def _(dve):
                def combine(i, r):
                    c = number(i, r)
                    wait(dve, loaded[r], turn(i) * 32 + 32)
                    dve.tensor_scalar(none[:, r], acc[:, r, :, D], 0.0, None, ALU.is_le).then_inc(combine_ops, 1)
                    wait(dve, combine_ops, c * 3 + 1)
                    dve.tensor_tensor(none[:, r], acc[:, r, :, D], none[:, r], ALU.add).then_inc(combine_ops, 1)
                    wait(dve, combine_ops, c * 3 + 2)
                    dve.reciprocal(gate_r[:, r], none[:, r]).then_inc(combine_ops, 1)
                    wait(dve, combine_ops, c * 3 + 3)
                    for q in range(Q):
                        dve.scalar_tensor_tensor(x1[:, r, q, :], acc[:, r, q, 0:D], gate_r[:, r, q:q + 1],
                                                 x1[:, r, q, :], ALU.mult, ALU.add).then_inc(combined, 1)
                    for q in range(Q):
                        wait(dve, combined, c * Q + (q + 1))
                        dve.bn_stats(stats[:, r, q, :], x1[:, r, q, :]).then_inc(stats_ops, 1)
                    wait(dve, stats_ops, c * 6 + Q)
                    dve.sem_inc(stats_seen, 1)
                    for q in range(Q):
                        op = dve.bn_aggr(mv[:, r, q, :], stats[:, r, q, :])
                    op.then_inc(stats_ops, 1)
                    wait(dve, stats_ops, c * 6 + 5)
                    dve.tensor_scalar(var_e[:, r], mv[:, r, :, 1], EPS, None, ALU.add).then_inc(stats_ops, 1)

                def shift_of(i, r):
                    c = number(i, r)
                    wait(dve, rooted, c + 1)
                    dve.scalar_tensor_tensor(shift[:, r], mv[:, r, :, 0], -1.0, rstd[:, r], ALU.mult,
                                             ALU.mult).then_inc(shifted, 1)

                dve.memset(neg_half[:], -0.5).then_inc(half_set, 1)

                def body(i):
                    for r in range(R + 1):
                        if r < R:
                            combine(i, r)
                        if r:
                            shift_of(i, r - 1)

                rounds(dve, body)

            @block.gpsimd
            def _(pool):
                pool.wait_ge(half_set, 1)

                def body(i):
                    for r in range(R):
                        wait(pool, stats_ops, number(i, r) * 6 + 6)
                        pool.tensor_tensor(rstd[:, r], var_e[:, r], neg_half[:], ALU.pow).then_inc(rooted, 1)

                rounds(pool, body)

            @block.scalar
            def _(act):
                def body(i):
                    for r in range(R):
                        c = number(i, r)
                        wait(act, shifted, c + 1)
                        if i is not None:
                            wait(act, left[r], turn(i) * 16)
                        for q in range(Q):
                            op = act.activation(out[:, r, q, :], x1[:, r, q, :], ACT.Identity,
                                                scale=rstd[:, r, q:q + 1], bias=shift[:, r, q:q + 1])
                        op.then_inc(normed, 1)
                        wait(act, normed, c + 1)
                        act.dma_start(rows_of(d["out"], c), out[:, r]).then_inc(left[r], 16)

                rounds(act, body)
                for r in range(R):
                    act.wait_ge(left[r], 16 * NI)


def host_layout(inputs):
    half = mybir.dt.np(BF16)
    g = {k.split("_", 2)[2]: np.ascontiguousarray(np.asarray(v)) for k, v in inputs.items()}
    x = g["x"]
    B, L, D = x.shape
    T = B * L
    DI, N = g["A_log"].shape
    R = g["W_dt"].shape[0]
    x = x.reshape(T, D)
    a = {}
    a["x"] = np.concatenate([np.zeros((CH, D), np.float32), x])
    xT = np.zeros((T // CH + 2, P, D // P, CH), np.float32)
    xT[:T // CH] = x.reshape(T // CH, CH, D // P, P).transpose(0, 3, 2, 1)
    a["xT"] = xT
    a["W_in"], a["W_dt"], a["W_out"] = g["W_in"], g["W_dt"], g["W_out"]
    a["W_x"] = np.concatenate([g["W_x"][:, R:]] * 3 + [g["W_x"][:, :R]], axis=1)
    a["W_r"] = np.ascontiguousarray(g["router_weight"].T)
    a["conv_w"], a["A_log"] = g["conv_w"], g["A_log"]
    for n in ("conv_b", "b_dt", "D_param"):
        a[n] = np.ascontiguousarray(g[n].reshape(DI // P, P).T)
    a["ident"] = np.eye(P, dtype=np.float32)
    pick = np.zeros((DP, 2 * N, P), half)
    for n in range(2 * N):
        pick[n::2 * N, n, :] = 1
    a["pick"] = pick
    a["nw_rows"] = np.ascontiguousarray(np.broadcast_to(g["norm_weight"], (P, D)))
    a["rb_rows"] = np.ascontiguousarray(np.broadcast_to(g["router_bias"], (P, len(g["router_bias"]))))
    a["router_bias"] = g["router_bias"]
    E = len(g["router_bias"])
    F = g["fc1_bias"].shape[1]
    J = P // E
    KT = max(1, -(-T // E)) // P
    NB = T // J // P
    part = np.arange(P)
    same = part[:, None] // J == part[None, :] // J
    a["same"] = same.astype(np.float32)
    a["before"] = (same & (part[:, None] < part[None, :])).astype(np.float32)
    a["ident_h"] = np.eye(P, dtype=half)
    bf = lambda v, shape: np.ascontiguousarray(np.broadcast_to(v, shape)).astype(half)
    a["iota_lo"] = bf(np.arange(P)[None, :, None], (P, P, J))
    a["iota_hi"] = bf(np.arange(1, KT + 1)[None, :, None], (P, KT, J))
    a["block_no"] = bf(np.arange(NB)[None, :, None] + np.arange(J)[None, None, :] * NB + Q, (P, NB, J))
    a["part_no"] = np.arange(P, dtype=np.float32)[:, None].copy()
    a["W1"] = np.ascontiguousarray(g["fc1_weight"].reshape(E, F, D // P, P).transpose(0, 3, 2, 1))
    a["W2"] = np.ascontiguousarray(g["fc2_weight"].reshape(E, D, F // P, P).transpose(0, 3, 2, 1))
    a["b1"] = np.ascontiguousarray(g["fc1_bias"].reshape(E, F // P, P).transpose(0, 2, 1))
    a["b2_rows"] = np.ascontiguousarray(np.broadcast_to(g["fc2_bias"][:, None, :], (E, P, D)))
    return a, (B, L, D)


def build(nc, d, T, D, E):
    for name, width in (("x1", D), ("table", D + E), ("acc", D + 1)):
        d[name] = nc.dram_tensor("rows_" + name, (T + CH, width), F32, kind="Internal").ap()
    d["logits"] = nc.dram_tensor("router_logits", (E, T + CH), F32, kind="Internal").ap()
    mamba_phase(nc, d)
    experts_phase(nc, d)
    final_phase(nc, d)


def kernel(**inputs):
    import concourse.bacc as bacc
    from concourse.bass_utils import run_bass_kernel_spmd

    arrays, shape = host_layout(inputs)
    B, L, D = shape
    E = arrays["router_bias"].shape[0]
    nc = bacc.Bacc("TRN2", target_bir_lowering=False, num_devices=1)
    d, given = {"seq": L}, {}
    for name, a in arrays.items():
        given["in_" + name] = a
        d[name] = nc.dram_tensor("in_" + name, a.shape, mybir.dt.from_np(a.dtype), kind="ExternalInput").ap()
    d["out"] = nc.dram_tensor("out_0", (B * L, D), F32, kind="ExternalOutput").ap()
    build(nc, d, B * L, D, E)
    r = run_bass_kernel_spmd(nc, [given], core_ids=[0])
    return r.results[0]["out_0"].reshape(B, L, D)
```
